# Optimizing a Trainium2 kernel written in Bass

```python
import numpy as np
import jax
import jax.numpy as jnp

def _softmax(x, axis=-1):
    return jax.nn.softmax(x, axis=axis)

def _gelu(x):
    return jax.nn.gelu(x, approximate=True)

def _silu(x):
    return jax.nn.silu(x)

def _sigmoid(x):
    return jax.nn.sigmoid(x)

def _layernorm(x, axis=-1, eps=1e-05):
    m = jnp.mean(x, axis=axis, keepdims=True)
    v = jnp.var(x, axis=axis, keepdims=True)
    return (x - m) / jnp.sqrt(v + eps)

def _scatter_add(tgt, idx, src, axis=0):
    return tgt.at[idx].add(src)

def _segment_sum(src, seg, n):
    return jax.ops.segment_sum(src, seg, n)
kernel_name = 'mk_prb_d1_jaxref_r4_046dae'

def setup_inputs(seed: int=0):
    np.random.seed(seed)
    _w = jnp.asarray

    def _L0_attn_setup():
        import jax, jax.numpy as jnp
        import numpy as np
        D_MODEL = 1024
        N_HEADS = 32
        HEAD_DIM = D_MODEL // N_HEADS
        CLIP_QKV = 8.0
        ALIBI_BIAS_MAX = 8.0
        LN_EPS = 1e-05

        def _alibi_slopes(n_heads: int, bias_max: float) -> jnp.ndarray:
            next_pow2 = 2 ** int(np.ceil(np.log2(n_heads)))
            m = np.arange(1, next_pow2 + 1, dtype=np.float32) * (bias_max / next_pow2)
            slopes = 1.0 / np.power(2.0, m)
            if next_pow2 != n_heads:
                slopes = np.concatenate([slopes[1::2], slopes[::2]])[:n_heads]
            return jnp.asarray(slopes)

        def _layer_norm(x, w, b):
            mu = jnp.mean(x, axis=-1, keepdims=True)
            var = jnp.mean(jnp.square(x - mu), axis=-1, keepdims=True)
            return (x - mu) * jax.lax.rsqrt(var + LN_EPS) * w + b
        key = jax.random.key(seed)
        ks = jax.random.split(key, 3)
        B, S = (1, 512)
        hidden_states = jax.random.normal(ks[0], (B, S, D_MODEL), dtype=jnp.float32)
        Wqkv = jax.random.normal(ks[1], (3 * D_MODEL, D_MODEL), dtype=jnp.float32) * 0.02
        Wout = jax.random.normal(ks[2], (D_MODEL, D_MODEL), dtype=jnp.float32) * 0.02
        return {'hidden_states': hidden_states, 'Wqkv': Wqkv, 'q_ln_w': jnp.ones((D_MODEL,), jnp.float32), 'q_ln_b': jnp.zeros((D_MODEL,), jnp.float32), 'k_ln_w': jnp.ones((D_MODEL,), jnp.float32), 'k_ln_b': jnp.zeros((D_MODEL,), jnp.float32), 'Wout': Wout}
    _L0_attn_in = _L0_attn_setup()

    def _L0_ffn_setup():
        import jax, jax.numpy as jnp
        import numpy as np

        def binarize_weight(W):
            alpha = jnp.mean(jnp.abs(W), axis=tuple(range(1, W.ndim)), keepdims=True)
            return alpha * jnp.sign(W)
        key = jax.random.key(seed)
        k1, k2, k3 = jax.random.split(key, 3)
        B, S, D_IN, D_OUT = (4, 512, 1024, 1024)
        x = jax.random.normal(k1, (B, S, D_IN), dtype=jnp.float32)
        weight_real = jax.random.normal(k2, (D_OUT, D_IN), dtype=jnp.float32)
        bias = jax.random.normal(k3, (D_OUT,), dtype=jnp.float32)
        return {'x': x, 'weight_real': weight_real, 'bias': bias}
    _L0_ffn_in = _L0_ffn_setup()
    _d = {'L0_attn_hidden_states': _L0_attn_in['hidden_states'], 'L0_attn_Wqkv': _L0_attn_in['Wqkv'], 'L0_attn_q_ln_w': _L0_attn_in['q_ln_w'], 'L0_attn_q_ln_b': _L0_attn_in['q_ln_b'], 'L0_attn_k_ln_w': _L0_attn_in['k_ln_w'], 'L0_attn_k_ln_b': _L0_attn_in['k_ln_b'], 'L0_attn_Wout': _L0_attn_in['Wout'], 'L0_ffn_weight_real': _L0_ffn_in['weight_real'], 'L0_ffn_bias': _L0_ffn_in['bias']}
    _x0 = _d['L0_attn_hidden_states']
    _d['L0_attn_hidden_states'] = jax.random.normal(jax.random.fold_in(jax.random.key(seed), 1), (2, 1024, 1024), dtype=_x0.dtype)
    del _x0
    return _d

def reference(L0_attn_hidden_states, L0_attn_Wqkv, L0_attn_q_ln_w, L0_attn_q_ln_b, L0_attn_k_ln_w, L0_attn_k_ln_b, L0_attn_Wout, L0_ffn_weight_real, L0_ffn_bias):

    def _L0_attn_ref(hidden_states, Wqkv, q_ln_w, q_ln_b, k_ln_w, k_ln_b, Wout):
        import jax, jax.numpy as jnp
        import numpy as np
        D_MODEL = 1024
        N_HEADS = 32
        HEAD_DIM = D_MODEL // N_HEADS
        CLIP_QKV = 8.0
        ALIBI_BIAS_MAX = 8.0
        LN_EPS = 1e-05

        def _alibi_slopes(n_heads: int, bias_max: float) -> jnp.ndarray:
            next_pow2 = 2 ** int(np.ceil(np.log2(n_heads)))
            m = np.arange(1, next_pow2 + 1, dtype=np.float32) * (bias_max / next_pow2)
            slopes = 1.0 / np.power(2.0, m)
            if next_pow2 != n_heads:
                slopes = np.concatenate([slopes[1::2], slopes[::2]])[:n_heads]
            return jnp.asarray(slopes)

        def _layer_norm(x, w, b):
            mu = jnp.mean(x, axis=-1, keepdims=True)
            var = jnp.mean(jnp.square(x - mu), axis=-1, keepdims=True)
            return (x - mu) * jax.lax.rsqrt(var + LN_EPS) * w + b
        B, S, _ = hidden_states.shape
        qkv = jnp.einsum('bsd,ed->bse', hidden_states, Wqkv)
        qkv = jnp.clip(qkv, -CLIP_QKV, CLIP_QKV)
        q, k, v = jnp.split(qkv, [D_MODEL, 2 * D_MODEL], axis=-1)
        q = _layer_norm(q, q_ln_w, q_ln_b)
        k = _layer_norm(k, k_ln_w, k_ln_b)
        q = q.reshape(B, S, N_HEADS, HEAD_DIM)
        k = k.reshape(B, S, N_HEADS, HEAD_DIM)
        v = v.reshape(B, S, N_HEADS, HEAD_DIM)
        scale = HEAD_DIM ** (-0.5)
        scores = jnp.einsum('bqhd,bkhd->bhqk', q, k) * scale
        slopes = _alibi_slopes(N_HEADS, ALIBI_BIAS_MAX)
        pos = jnp.arange(S)
        rel = (pos[None, :] - pos[:, None]).astype(jnp.float32)
        scores = scores + slopes[None, :, None, None] * rel[None, None]
        causal = pos[None, :] <= pos[:, None]
        scores = jnp.where(causal[None, None], scores, jnp.float32(-1e+30))
        probs = jax.nn.softmax(scores, axis=-1)
        out = jnp.einsum('bhqk,bkhd->bqhd', probs, v).reshape(B, S, D_MODEL)
        return jnp.einsum('bsd,ed->bse', out, Wout)

    def _L0_ffn_ref(x, weight_real, bias):
        import jax, jax.numpy as jnp
        import numpy as np

        def binarize_weight(W):
            alpha = jnp.mean(jnp.abs(W), axis=tuple(range(1, W.ndim)), keepdims=True)
            return alpha * jnp.sign(W)
        W = binarize_weight(weight_real)
        return jnp.einsum('bsi,oi->bso', x, W) + bias
    x = L0_attn_hidden_states
    xn = _layernorm(x, axis=-1)
    x = x + _L0_attn_ref(xn, L0_attn_Wqkv, L0_attn_q_ln_w, L0_attn_q_ln_b, L0_attn_k_ln_w, L0_attn_k_ln_b, L0_attn_Wout) + _L0_ffn_ref(xn, L0_ffn_weight_real, L0_ffn_bias)
    return x

_drawn_inputs = setup_inputs


def setup_inputs(seed=0):
    import zlib

    import numpy as np

    out = dict(_drawn_inputs(seed))
    spreads = {'L0_attn_q_ln_w': (1.0, 0.6),
     'L0_attn_q_ln_b': (0.0, 0.8),
     'L0_attn_k_ln_w': (1.0, 0.6),
     'L0_attn_k_ln_b': (0.0, 0.8)}
    factors = {'L0_attn_Wqkv': 8.0, 'L0_attn_Wout': 8.0}
    for name, (base, spread) in spreads.items():
        noise = np.random.default_rng([zlib.crc32(name.encode()), seed]).standard_normal(out[name].shape)
        drawn = base * np.exp(spread * noise) if base else spread * noise
        out[name] = jnp.asarray(drawn.astype(out[name].dtype))
    for name, factor in factors.items():
        out[name] = (out[name] * factor).astype(out[name].dtype)
    return out
```

```python
from contextlib import ExitStack

import concourse.bass as bass
from concourse import mybir

F32, F16, BF16, U16 = mybir.dt.float32, mybir.dt.float16, mybir.dt.bfloat16, mybir.dt.uint16
ALU = mybir.AluOpType
ACT = mybir.ActivationFunctionType
AX = mybir.AxisListType.X

P = 128
BATCH, SEQ, DM = 2, 1024, 1024
HEADS, DH = 32, 32
TOK = BATCH * SEQ
NT = TOK // P
KT = DM // P
QT = SEQ // P
HALF = 512
LN_EPS = 1e-5
CLIP = 8.0
SX = 256.0
SW = 256.0
VW = 2 * DH + 1

RING = 2


def ready(n):
    return n + 1 + RING


def slot_free(n):
    return n + 1


def stored(j):
    return 16 * j + 16


def tile_loop(eng, step):
    step(0, 0, 0, first=True)
    with eng.Fori(0, NT // 2 - 1) as it:
        step(it * 2 + 1, 1, it)
        step(it * 2 + 2, 0, it + 1)
    step(NT - 1, 1, NT // 2 - 1)


def build_program(nc, x, wqkv_t, wout_t, wffn_t, ffn_bias, q_w, q_b, k_w, k_b,
                  ident_h, ident_b, mask_nat, mask_tr, q_extra, k_extra, out):
    q_scr = nc.dram_tensor("q_scr", [HEADS, 2 * DH, TOK], F16, kind="Internal").ap()
    k_scr = nc.dram_tensor("k_scr", [HEADS, 2 * DH, TOK], F16, kind="Internal").ap()
    v_scr = nc.dram_tensor("v_scr", [NT, P, HEADS * VW], F16, kind="Internal").ap()
    base_scr = nc.dram_tensor("base_scr", [NT, P, DM], F32, kind="Internal").ap()
    wo_scr = nc.dram_tensor("wo_scr", [P, KT * 2 * DM], F16, kind="Internal").ap()

    ctx = ExitStack()
    with ctx:
        WORDS = 52992
        arena = ctx.enter_context(nc.sbuf_tensor("arena", [P, WORDS], F32))
        small = ctx.enter_context(nc.sbuf_tensor("small", [P, 128], F32))

        def f32(at, n):
            return arena[:, at:at + n]

        def f16(at, n):
            return arena[:, at:at + n // 2].bitcast(F16)

        at = 0
        idh = f16(at, P); at += P // 2
        idb = arena[:, at:at + P // 2].bitcast(BF16); at += P // 2
        mnat = arena[:, at:at + P // 2].bitcast(BF16); at += P // 2
        mtr = arena[:, at:at + P // 2].bitcast(BF16); at += P // 2
        ones = f32(at, P); at += P
        START = at

        at = START
        xnt = f16(at, KT * 2 * TOK).rearrange("p (k s t) -> p k s t", k=KT, s=2); at += KT * TOK
        wsl = [f16(at + s * KT * DM, KT * 2 * DM).rearrange("p (k s n) -> p k s n", k=KT, s=2)
               for s in range(2)]; at += 2 * KT * DM
        wo_part = f16(START + KT * TOK, KT * 2 * DM)
        stage = [f32(at + s * HALF, HALF) for s in range(2)]; at += 2 * HALF
        absw = [f32(at + s * HALF, HALF) for s in range(2)]; at += 2 * HALF
        xc = [f32(at + s * DM, DM) for s in range(2)]; at += 2 * DM
        u = [f32(at + s * DM, DM) for s in range(2)]; at += 2 * DM
        split_at = at
        xh = [f16(split_at + s * DM, DM) for s in range(2)]
        xl = [f16(split_at + s * DM + DM // 2, DM) for s in range(2)]
        qhl = [f16(split_at + s * DM, 2 * DM).rearrange("p (h s d) -> p h s d", h=HEADS, s=2)
               for s in range(2)]; at += 2 * DM
        turn_at = at
        fb = [f32(turn_at + s * DM, DM) for s in range(2)]
        xb = [f32(turn_at + (2 + s) * DM, DM) for s in range(2)]
        tbuf = [f16(turn_at + s * DM, 2 * DM).rearrange("p (j t) -> p j t", j=HEADS // 2)
                for s in range(2)]; at += 4 * DM
        vst_at = at
        alpha = f32(vst_at, DM)
        bias = f32(vst_at + DM, DM)
        vst = [f16(vst_at + s * HEADS * VW // 2, HEADS * VW).rearrange("p (h c) -> p h c", h=HEADS)
               for s in range(2)]; at += HEADS * VW
        ln_w = {"q": f32(at, DM), "k": f32(at + DM, DM)}; at += 2 * DM
        ln_b = {"q": f32(at, DM), "k": f32(at + DM, DM)}; at += 2 * DM
        assert at <= WORDS, at

        at = START
        vall = f16(at, NT * HEADS * VW).rearrange("p (t h c) -> p t h c", t=NT, h=HEADS)
        vflat = f16(at, NT * HEADS * VW).rearrange("p (t n) -> p t n", t=NT); at += NT * HEADS * VW // 2
        o_at = at
        oall = f32(at, NT * DM).rearrange("p (t n) -> p t n", t=NT); at += NT * DM
        PCOLS = sum(SEQ - P * t for t in range(QT))
        OFF = [sum(SEQ - P * s for s in range(t)) for t in range(QT)]
        p_at = at
        p32 = [f32(at + s * PCOLS, PCOLS) for s in range(2)]; at += 2 * PCOLS
        ph = [v.bitcast(BF16)[:, 1:2 * PCOLS:2] for v in p32]
        pl = [f16(at + s * PCOLS // 2, PCOLS) for s in range(2)]; at += PCOLS
        STACKS = 4
        qs = [f16(at + s * SEQ // 2, SEQ) for s in range(STACKS)]; at += STACKS * SEQ // 2
        ks = [f16(at + s * SEQ // 2, SEQ) for s in range(STACKS)]; at += STACKS * SEQ // 2
        osum = [f32(at + s * 4 * DH, 4 * DH).rearrange("p (i d) -> p i d", i=4) for s in range(2)]
        at += 8 * DH
        negm = [f16(at + s * 8, 16) for s in range(2)]; at += 16
        rrow = [f16(at + s * P // 2, P) for s in range(2)]; at += P
        assert at <= WORDS, at

        at = START
        wo_flat = f16(at, KT * 2 * DM)
        wo = wo_flat.rearrange("p (k s n) -> p k s n", k=KT, s=2)
        at = p_at
        oh = [f16(at + s * DM, DM) for s in range(2)]
        ol = [f16(at + s * DM + DM // 2, DM) for s in range(2)]; at += 2 * DM
        ot = [f16(at + s * DM, 2 * DM).rearrange("p (k s t) -> p k s t", k=KT, s=2) for s in range(2)]
        at += 2 * DM
        basec = [f32(at + s * DM, DM) for s in range(2)]; at += 2 * DM
        outc = [f32(at + s * DM, DM) for s in range(2)]; at += 2 * DM
        assert at <= WORDS, at

        bst = [small[:, 12 * s:12 * s + 12] for s in range(2)]
        mv = [small[:, 24 + 2 * s:26 + 2 * s] for s in range(2)]
        var_eps = [small[:, 28 + s:29 + s] for s in range(2)]
        rs = [small[:, 30 + s:31 + s] for s in range(2)]
        nb = [small[:, 32 + s:33 + s] for s in range(2)]
        recd = [small[:, 36 + 4 * s:40 + 4 * s] for s in range(2)]
        expo, eps_x, eps_qk, plus_sx, minus_sx = (small[:, c:c + 1] for c in range(44, 49))
        plain = [small[:, 49 + s:50 + s] for s in range(2)]
        minus = [small[:, 51 + s:52 + s] for s in range(2)]

        ps = ctx.enter_context(nc.psum_tensor("ps", [P, 8, HALF], F32))

        def banks(b, n):
            return ps[:, b:b + n, :].rearrange("p b n -> p (b n)")

        def bank16(b):
            return ps[:, b, :].bitcast(F16)

        def sem(name):
            return ctx.enter_context(nc.semaphore(name))

        const_ld = sem("const_ld")
        bc_ld = sem("bc_ld")
        x_ld = [sem(f"x_ld{s}") for s in range(2)]
        w_ld = [sem(f"w_ld{s}") for s in range(2)]
        base_st = [sem(f"base_st{s}") for s in range(2)]
        t_st = [sem(f"t_st{s}") for s in range(2)]
        v_st = [sem(f"v_st{s}") for s in range(2)]
        wo_st = sem("wo_st")
        v_ld = sem("v_ld")
        head_ld = [sem(f"head_ld{s}") for s in range(STACKS)]
        extra_ld = sem("extra_ld")
        r_ld = [sem(f"r_ld{s}") for s in range(2)]
        wo_ld = sem("wo_ld")
        base_ld = [sem(f"base_ld{s}") for s in range(2)]
        out_st = [sem(f"out_st{s}") for s in range(2)]
        setup = sem("setup")
        ones_set = sem("ones_set")
        alpha_set = sem("alpha_set")
        nb_part = sem("nb_part")
        w_hi = sem("w_hi")
        w_lo = sem("w_lo")
        abs_used = sem("abs_used")
        bn_part = sem("bn_part")
        stats = sem("stats")
        ve_done = sem("ve_done")
        pow_done = sem("pow_done")
        rstd_done = sem("rstd_done")
        xn_done = sem("xn_done")
        xh_done = sem("xh_done")
        xl_done = sem("xl_done")
        xt_done = sem("xt_done")
        xth_out = sem("xth_out")
        xtl_out = sem("xtl_out")
        xb_done = sem("xb_done")
        base_done = sem("base_done")
        mm_done = sem("mm_done")
        mm_out = sem("mm_out")
        uw_done = sem("uw_done")
        u_done = sem("u_done")
        hi_done = sem("hi_done")
        lo_done = sem("lo_done")
        qt_done = sem("qt_done")
        qt_out = sem("qt_out")
        vh_done = sem("vh_done")
        vl_done = sem("vl_done")
        ones_v = sem("ones_v")
        nat_done = sem("nat_done")
        nat_out = sem("nat_out")
        negm_done = sem("negm_done")
        st_done = sem("st_done")
        exp_done = sem("exp_done")
        plp_done = sem("plp_done")
        plv_done = sem("plv_done")
        pv_done = sem("pv_done")
        ocopy = sem("ocopy")
        rec_done = sem("rec_done")
        o_out = sem("o_out")
        o_sum = sem("o_sum")
        oh_done = sem("oh_done")
        ol_done = sem("ol_done")
        ott_done = sem("ott_done")
        oth_out = sem("oth_out")
        otl_out = sem("otl_out")
        c_done = sem("c_done")
        c_out = sem("c_out")

        w_src = [wffn_t, wqkv_t[:, 0:DM], wqkv_t[:, DM:2 * DM], wqkv_t[:, 2 * DM:3 * DM], wout_t]
        F, Q, K, V, WO = range(5)
        LNQ = {Q: "q", K: "k"}
        STEPS = 2 * HEADS
        NAT = [[(0, 0, P, 0), (1, 0, 2 * P, P)], [(2, 0, 3 * P, 0)], [(3, 0, 4 * P, 0)]]
        for i in range(4, QT):
            NAT += [[(i, 0, HALF, 0)], [(i, HALF, P * (i + 1) - HALF, 0)]]
        NB = len(NAT) + 1
        assert NB % 2 == 0
        SCALE = float(DH) ** -0.5

        def step_no(n, per_step=1, more=0):
            return n[0] * (4 * per_step) + (n[1] * per_step + more)

        block = ctx.enter_context(nc.Block())

        @block.sync
        def _(sp):
            for dst, src in ((idh, ident_h), (idb.bitcast(U16), ident_b), (mnat.bitcast(U16), mask_nat),
                             (mtr.bitcast(U16), mask_tr)):
                sp.dma_start(dst, src).then_inc(const_ld, 16)

            def load_x(t, p, j):
                sp.wait_ge(xn_done, slot_free(t))
                sp.wait_ge(xb_done, slot_free(t))
                sp.dma_start(xc[p], x[bass.ds(t * P, P), :]).then_inc(x_ld[p], 16)

            def load_w(blk, t, p, j):
                sp.wait_ge(w_hi, slot_free(t + NT * blk))
                sp.wait_ge(w_lo, slot_free(t + NT * blk))
                sp.dma_start(stage[p], w_src[blk][bass.ds(j * P, P), p * HALF:(p + 1) * HALF])\
                  .then_inc(w_ld[p], 16)

            def store_base(t, p, j):
                sp.wait_ge(base_done, ready(t))
                sp.dma_start(base_scr[bass.ds(t, 1), :, :].rearrange("o p n -> p (o n)"), fb[p])\
                  .then_inc(base_st[p], 16)

            load_x(0, 0, 0)
            load_w(F, 0, 0, 0)
            load_w(F, 1, 1, 0)
            for dst, src in ((bias, ffn_bias), (ln_w["q"], q_w), (ln_b["q"], q_b),
                             (ln_w["k"], k_w), (ln_b["k"], k_b)):
                sp.dma_start(dst, src.partition_broadcast(P)).then_inc(bc_ld, 16)
            with sp.Fori(1, KT) as j:
                for p in range(2):
                    load_w(F, j * 2 + p, p, j)
            for t in range(2):
                if t:
                    load_x(t, t, 0)
                load_w(Q, t, t, 0)
            with sp.Fori(1, NT // 2) as j:
                for p in range(2):
                    load_x(j * 2 + p, p, j)
                    load_w(Q, j * 2 + p, p, j)
                    store_base((j - 1) * 2 + p, p, j - 1)
            for p in range(2):
                store_base(NT - 2 + p, p, NT // 2 - 1)
            for blk in (K, V):
                with sp.Fori(0, NT // 2) as j:
                    for p in range(2):
                        load_w(blk, j * 2 + p, p, j)

            def v_step(t, p, j, first=False):
                load_w(WO, t, p, j)
                if not first:
                    store_v(t - 1, 1 - p)

            def store_v(t, p):
                sp.wait_ge(vl_done, ready(t))
                sp.dma_start(v_scr[bass.ds(t, 1), :, :].rearrange("o p n -> p (o n)"),
                             vst[p].rearrange("p h c -> p (h c)")).then_inc(v_st[p], 16)

            tile_loop(sp, v_step)
            store_v(NT - 1, 1)
            sp.wait_ge(w_lo, ready(NT * 5 - 1))
            sp.dma_start(wo_scr, wo_part).then_inc(wo_st, 16)

            for s in range(2):
                sp.wait_ge(v_st[s], stored(NT // 2))
                sp.wait_ge(t_st[s], stored(NT))
            sp.wait_ge(wo_st, 16)
            sp.wait_ge(mm_done, NT * 4)

            def load_head(n):
                s, b, h = n[1] % STACKS, n[1] % 2, n[0] * 2 + n[1] // 2
                toks = slice(b * SEQ, (b + 1) * SEQ)
                sp.wait_ge(st_done, step_no(n, QT, QT))
                hq = q_scr[bass.ds(h, 1), :, toks].rearrange("o r t -> (o r) t")
                hk = k_scr[bass.ds(h, 1), :, toks].rearrange("o r t -> (o r) t")
                ex = k_extra[bass.ds(h, 1), :, :].rearrange("o r t -> (o r) t")
                sp.dma_start(ks[s][DH:2 * DH], hk[0:DH]).then_inc(head_ld[s], 16)
                sp.dma_start(ks[s][2 * DH:4 * DH], hk).then_inc(head_ld[s], 16)
                sp.dma_start(ks[s][0:4], ex).then_inc(head_ld[s], 16)
                sp.dma_start(qs[s][DH:3 * DH], hq).then_inc(head_ld[s], 16)
                sp.dma_start(qs[s][3 * DH:4 * DH], hq[0:DH]).then_inc(head_ld[s], 16)
                sp.dma_start(qs[s][0:1], q_extra[0:1]).then_inc(head_ld[s], 16)

            def load_row(n):
                sp.wait_ge(nat_out, step_no(n, NB, ready(NB - 1)))
                sp.dma_start(qs[n[1] % STACKS][0:1, :],
                             rrow[n[1] % 2][0:QT, :])\
                  .then_inc(r_ld[n[1] % 2], 16)

            for s in range(STACKS):
                sp.dma_start(ks[s][0:DH], q_extra).then_inc(extra_ld, 16)
                sp.dma_start(qs[s][0:DH], q_extra).then_inc(extra_ld, 16)
            sp.wait_ge(extra_ld, 16 * 2 * STACKS)
            for r in range(2):
                load_head((0, r))
            for t0 in range(0, NT, 4):
                sp.dma_start(vflat[:, t0:t0 + 4, :], v_scr[t0:t0 + 4].rearrange("t p n -> p t n"))\
                  .then_inc(v_ld, 16)
            for r in range(2, 4):
                load_head((0, r))
            load_row((0, 0))
            load_row((0, 1))
            with sp.Fori(0, STEPS // 4 - 1) as i:
                for r in range(4):
                    load_head((i, 4 + r))
                    load_row((i, 2 + r))
            load_row((0, STEPS - 2))
            load_row((0, STEPS - 1))

            sp.wait_ge(pv_done, 2 * STEPS + 4)
            for c in range(2):
                n = KT * DM
                sp.dma_start(wo_flat[:, c * n:(c + 1) * n], wo_scr[:, c * n:(c + 1) * n])\
                  .then_inc(wo_ld, 16)

            def load_base(t, p):
                sp.wait_ge(c_out, slot_free(t))
                sp.dma_start(basec[p], base_scr[bass.ds(t, 1), :, :].rearrange("o p n -> p (o n)"))\
                  .then_inc(base_ld[p], 16)

            def store_out(t, p):
                sp.wait_ge(c_out, ready(t))
                sp.dma_start(out[bass.ds(t * P, P), :], outc[p]).then_inc(out_st[p], 16)

            load_base(0, 0)
            load_base(1, 1)
            with sp.Fori(1, NT // 2) as j:
                for p in range(2):
                    load_base(j * 2 + p, p)
                    store_out((j - 1) * 2 + p, p)
            for p in range(2):
                store_out(NT - 2 + p, p)
            for p in range(2):
                sp.wait_ge(out_st[p], stored(NT // 2))

        @block.gpsimd
        def _(pool):
            for s in (rstd_done, xb_done, lo_done, plp_done):
                pool.sem_inc(s, RING)
            for col, value in ((expo, -0.5), (eps_x, LN_EPS), (eps_qk, LN_EPS * (SX * SW) ** 2),
                               (plus_sx, SX), (minus_sx, -SX)):
                nc.gpsimd.memset(col, value).then_inc(setup, 1)
            pool.wait_ge(setup, 5)

            def variance_plus(g, p, eps):
                pool.wait_ge(stats, ready(g))
                nc.gpsimd.tensor_tensor(var_eps[p], mv[p][:, 1:2], eps, ALU.add).then_inc(ve_done, 1)
                pool.wait_ge(ve_done, g + 1)

            def f_step(t, p, j, first=False):
                variance_plus(t, p, eps_x)
                nc.gpsimd.tensor_tensor(plain[p], var_eps[p], expo, ALU.pow).then_inc(pow_done, 1)
                pool.wait_ge(pow_done, t + 1)
                pool.wait_ge(xn_done, slot_free(t))
                nc.gpsimd.tensor_tensor(minus[p], plain[p], minus_sx, ALU.mult)
                nc.gpsimd.tensor_tensor(rs[p], plain[p], plus_sx, ALU.mult).then_inc(nb_part, 1)
                pool.wait_ge(nb_part, t + 1)
                nc.gpsimd.tensor_tensor(nb[p], mv[p][:, 0:1], minus[p], ALU.mult).then_inc(rstd_done, 1)
                pool.wait_ge(bc_ld, 16 * 5)
                pool.wait_ge(base_done, slot_free(t))
                nc.gpsimd.tensor_tensor(xb[p], xc[p], bias, ALU.add).then_inc(xb_done, 1)

            tile_loop(pool, f_step)

            for blk in (Q, K):
                def qk_step(t, p, j, first=False):
                    g, q = t + NT * blk, t + NT * (blk - 1)
                    variance_plus(g, p, eps_qk)
                    pool.wait_ge(u_done, slot_free(q))
                    nc.gpsimd.tensor_tensor(rs[p], var_eps[p], expo, ALU.pow).then_inc(rstd_done, 1)
                    pool.wait_ge(hi_done, ready(q))
                    nc.gpsimd.tensor_tensor(qhl[p][:, :, 1, :],
                                            u[p].rearrange("p (h d) -> p h d", h=HEADS),
                                            qhl[p][:, :, 0, :], ALU.subtract).then_inc(lo_done, 1)

                tile_loop(pool, qk_step)

            for s in range(2):
                pool.wait_ge(base_st[s], stored(NT // 2))
            for s in range(2):
                nc.gpsimd.memset(vst[s][:, :, 2 * DH:VW], 1.0).then_inc(ones_v, 1)

            def low_parts(n):
                p = n[1] % 2
                for t in range(4):
                    pool.wait_ge(exp_done, step_no(n, QT, ready(t)))
                    cols = slice(OFF[t], OFF[t] + SEQ - P * t)
                    nc.gpsimd.tensor_tensor(pl[p][:, cols], p32[p][:, cols], ph[p][:, cols],
                                            ALU.subtract).then_inc(plp_done, 1)

            with pool.Fori(0, STEPS // 4) as i:
                for r in range(4):
                    low_parts((i, r))

        @block.scalar
        def _(act):
            for s in (w_hi, xn_done, xh_done, xth_out, hi_done, qt_out, vh_done, exp_done,
                      ocopy, oh_done, oth_out):
                act.sem_inc(s, RING)
            for s in (*t_st, *v_st):
                act.sem_inc(s, 16)

            def split_hi(blk, t, p, j):
                act.wait_ge(w_ld[p], j * 16 + (16 * KT * blk + 16))
                dst = wsl[blk % 2][:, bass.ds(j, 1), 0, p * HALF:(p + 1) * HALF]\
                    .rearrange("p o n -> p (o n)")
                if blk == F:
                    nc.scalar.activation(dst, stage[p], ACT.Sign).then_inc(w_hi, 1)
                else:
                    nc.scalar.activation(dst, stage[p], ACT.Copy, scale=SW).then_inc(w_hi, 1)

            with act.Fori(0, KT) as j:
                for p in range(2):
                    split_hi(F, j * 2 + p, p, j)

            def f_step(t, p, j, first=False):
                split_hi(Q, t, p, j)
                act.wait_ge(x_ld[p], j * 16 + 16)
                act.wait_ge(rstd_done, ready(t))
                act.wait_ge(xl_done, slot_free(t))
                nc.scalar.activation(u[p], xc[p], ACT.Identity, bias=nb[p], scale=rs[p])\
                  .then_inc(xn_done, 1)
                act.wait_ge(xn_done, ready(t))
                act.wait_ge(xt_done, slot_free(t))
                nc.scalar.activation(xh[p], u[p], ACT.Copy).then_inc(xh_done, 1)
                act.wait_ge(xt_done, ready(t))
                nc.scalar.activation(xnt[:, :, 0, bass.ds(t * P, P)],
                                     bank16(4 + 2 * p).rearrange("p (k t) -> p k t", k=KT), ACT.Copy)\
                  .then_inc(xth_out, 1)

            tile_loop(act, f_step)

            def turn_out(scr, q, t, p, stores):
                act.wait_ge(qt_done, ready(q))
                act.wait_ge(t_st[p], stored(stores))
                half = HEADS // 4
                for c in range(2):
                    ins = nc.scalar.activation(
                        tbuf[p][:, c * half:(c + 1) * half, :],
                        bank16(4 + 2 * p + c).rearrange("p (j t) -> p j t", t=P), ACT.Copy)
                ins.then_inc(qt_out, 1)
                act.wait_ge(qt_out, ready(q))
                dst = scr.rearrange("h r t -> (h r) t").rearrange("(j p) t -> p j t", p=P)
                act.dma_start(dst[:, :, bass.ds(t * P, P)], tbuf[p]).then_inc(t_st[p], 16)

            for s in range(2):
                act.wait_ge(base_st[s], stored(NT // 2))

            for blk in (Q, K):
                act.wait_ge(mm_done, NT * blk)

                def qk_step(t, p, j, first=False):
                    q = t + NT * (blk - 1)
                    split_hi(blk + 1, t, p, j)
                    if not first:
                        before = (j if p else j - 1) + NT // 2 * (blk - 1)
                        turn_out({Q: q_scr, K: k_scr}[blk], q - 1, t - 1, 1 - p, before)
                    elif blk == K:
                        turn_out(q_scr, NT - 1, NT - 1, 1, NT // 2 - 1)
                    act.wait_ge(u_done, ready(q))
                    act.wait_ge(qt_done, slot_free(q))
                    nc.scalar.activation(qhl[p][:, :, 0, :],
                                         u[p].rearrange("p (h d) -> p h d", h=HEADS),
                                         ACT.Copy).then_inc(hi_done, 1)

                tile_loop(act, qk_step)

            act.wait_ge(mm_done, NT * V)
            act.wait_ge(ones_v, 2)

            def v_step(t, p, j, first=False):
                split_hi(WO, t, p, j)
                if first:
                    turn_out(k_scr, 2 * NT - 1, NT - 1, 1, NT - 1)
                act.wait_ge(mm_out, ready(t + NT * V))
                act.wait_ge(v_st[p], stored(j))
                nc.scalar.activation(vst[p][:, :, 0:DH], xc[p].rearrange("p (h d) -> p h d", h=HEADS),
                                     ACT.Copy, scale=1.0 / SW).then_inc(vh_done, 1)

            tile_loop(act, v_step)

            act.wait_ge(extra_ld, 16 * 2 * STACKS)

            def exps(n, t):
                p = n[1] % 2
                act.wait_ge(st_done, step_no(n, QT, t + 1 + STACKS * QT))
                if t == 0:
                    act.wait_ge(pv_done, step_no(n, 2, 2))
                first = P * t if t < 4 else P * t - HALF
                src = banks(2 + 2 * (t % 2), 2 if t < 4 else 1)
                w = SEQ - P * t
                nc.scalar.activation(p32[p][:, OFF[t]:OFF[t] + w], src[:, first:first + w], ACT.Exp,
                                     scale=SCALE).then_inc(exp_done, 1)

            def low_columns(n, half):
                act.wait_ge(pv_done, step_no(n, 2, half + 5))
                act.wait_ge(o_out, step_no(n, 2, slot_free(half)))
                nc.scalar.activation(osum[half], ps[:, 6 + half, 0:4 * VW]
                                     .rearrange("p (i c) -> p i c", c=VW)[:, :, DH:2 * DH], ACT.Copy)\
                  .then_inc(ocopy, 1)

            def b_step(n, first=False):
                for t in range(QT):
                    exps(n, t)
                    if not first and t in (5, 7):
                        low_columns((n[0], n[1] - 1), (t - 5) // 2)

            b_step((0, 0), first=True)
            b_step((0, 1))
            with act.Fori(0, STEPS // 4 - 1) as i:
                for r in range(4):
                    b_step((i, 2 + r))
            b_step((0, STEPS - 2))
            b_step((0, STEPS - 1))
            for half in range(2):
                low_columns((0, STEPS - 1), half)

            act.wait_ge(o_out, ready(2 * STEPS - 1))

            def c_step(t, p, j, first=False):
                act.wait_ge(ott_done, slot_free(t))
                nc.scalar.activation(oh[p], oall[:, bass.ds(t, 1), :].rearrange("p o n -> p (o n)"),
                                     ACT.Copy).then_inc(oh_done, 1)
                act.wait_ge(ott_done, ready(t))
                act.wait_ge(c_done, slot_free(t))
                nc.scalar.activation(ot[p][:, :, 0, :],
                                     bank16(4 + 2 * p).rearrange("p (k t) -> p k t", k=KT),
                                     ACT.Copy).then_inc(oth_out, 1)

            tile_loop(act, c_step)

        @block.vector
        def _(dve):
            for s in (w_lo, stats, xl_done, xtl_out, base_done, mm_out, u_done, vl_done, nat_out,
                      o_out, ol_done, otl_out, c_out):
                dve.sem_inc(s, RING)
            for s in (*base_st, *out_st, *r_ld):
                dve.sem_inc(s, 16)
            nc.vector.memset(ones, 1.0).then_inc(ones_set, 1)

            def split_lo(blk, t, p, j):
                g = t + NT * blk
                dve.wait_ge(w_hi, ready(g))
                if blk == F:
                    dve.wait_ge(w_ld[p], j * 16 + 16)
                    dve.wait_ge(abs_used, slot_free(t))
                    nc.vector.scalar_tensor_tensor(absw[p], stage[p], -1.0, stage[p], ALU.mult, ALU.max)\
                      .then_inc(w_lo, 1)
                    return
                part = [wsl[blk % 2][:, bass.ds(j, 1), s, p * HALF:(p + 1) * HALF]
                        .rearrange("p o n -> p (o n)") for s in range(2)]
                nc.vector.scalar_tensor_tensor(part[1], stage[p], SW, part[0], ALU.mult, ALU.subtract)\
                  .then_inc(w_lo, 1)

            def statistics(g, p, between):
                for c in range(2):
                    ins = nc.vector.bn_stats(bst[p][:, 6 * c:6 * c + 6], xc[p][:, c * HALF:(c + 1) * HALF])
                ins.then_inc(bn_part, 1)
                dve.wait_ge(bn_part, g + 1)
                dve.wait_ge(rstd_done, slot_free(g))
                between()
                nc.vector.bn_aggr(mv[p], bst[p]).then_inc(stats, 1)

            with dve.Fori(0, KT) as j:
                for p in range(2):
                    split_lo(F, j * 2 + p, p, j)
            dve.wait_ge(abs_used, ready(NT - 1))
            nc.vector.tensor_scalar(alpha, banks(2, 2), 1.0 / (DM * SX), None, ALU.mult)\
              .then_inc(alpha_set, 1)
            dve.wait_ge(alpha_set, 1)

            def f_out(t, p, j):
                dve.wait_ge(mm_done, t + 1)
                dve.wait_ge(base_st[p], stored(j))
                nc.vector.tensor_tensor(fb[p], banks(2 * p, 2), alpha, ALU.mult).then_inc(mm_out, 1)
                dve.wait_ge(mm_out, ready(t))
                dve.wait_ge(xb_done, ready(t))
                nc.vector.tensor_tensor(fb[p], fb[p], xb[p], ALU.add).then_inc(base_done, 1)

            def f_step(t, p, j, first=False):
                dve.wait_ge(x_ld[p], j * 16 + 16)
                statistics(t, p, lambda: split_lo(Q, t, p, j))
                dve.wait_ge(xh_done, ready(t))
                nc.vector.tensor_tensor(xl[p], u[p], xh[p], ALU.subtract).then_inc(xl_done, 1)
                dve.wait_ge(xt_done, ready(t))
                nc.vector.tensor_copy(xnt[:, :, 1, bass.ds(t * P, P)],
                                      bank16(5 + 2 * p).rearrange("p (k t) -> p k t", k=KT))\
                  .then_inc(xtl_out, 1)
                if not first:
                    f_out(t - 1, 1 - p, j if p else j - 1)

            tile_loop(dve, f_step)
            f_out(NT - 1, 1, NT // 2 - 1)

            def clipped(g, p):
                dve.wait_ge(mm_done, g + 1)
                lim = CLIP * SX * SW
                nc.vector.tensor_scalar(xc[p], banks(2 * p, 2), lim, -lim, ALU.min, ALU.max)\
                  .then_inc(mm_out, 1)

            dve.wait_ge(xn_done, ready(NT - 1))
            dve.wait_ge(xb_done, ready(NT - 1))
            dve.wait_ge(bc_ld, 16 * 5)
            for blk in (Q, K):
                def qk_step(t, p, j, first=False):
                    g, q = t + NT * blk, t + NT * (blk - 1)
                    w, b = ln_w[LNQ[blk]], ln_b[LNQ[blk]]
                    clipped(g, p)
                    dve.wait_ge(mm_out, ready(g))
                    statistics(g, p, lambda: split_lo(blk + 1, t, p, j))
                    dve.wait_ge(rstd_done, ready(g))
                    dve.wait_ge(lo_done, slot_free(q))
                    nc.vector.scalar_tensor_tensor(u[p], xc[p], mv[p][:, 0:1], w, ALU.subtract, ALU.mult)\
                      .then_inc(uw_done, 1)
                    dve.wait_ge(uw_done, q + 1)
                    nc.vector.scalar_tensor_tensor(u[p], u[p], rs[p], b, ALU.mult, ALU.add)\
                      .then_inc(u_done, 1)

                tile_loop(dve, qk_step)

            def v_step(t, p, j, first=False):
                dve.wait_ge(vh_done, slot_free(t))
                clipped(t + NT * V, p)
                split_lo(WO, t, p, j)
                dve.wait_ge(vh_done, ready(t))
                nc.vector.scalar_tensor_tensor(vst[p][:, :, DH:2 * DH],
                                               xc[p].rearrange("p (h d) -> p h d", h=HEADS),
                                               1.0 / SW, vst[p][:, :, 0:DH], ALU.mult, ALU.subtract)\
                  .then_inc(vl_done, 1)

            tile_loop(dve, v_step)

            dve.wait_ge(extra_ld, 16 * 2 * STACKS)

            def maxima(n, c):
                p = n[1] % 2
                dve.wait_ge(nat_done, step_no(n, NB, c + 1))
                for i, key, width, col in NAT[c]:
                    at = i if key == 0 else i + 4
                    ins = nc.vector.tensor_reduce(negm[p][:, at:at + 1], ps[:, c % 2, col:col + width],
                                                  AX, ALU.max, negate=True)
                ins.then_inc(nat_out, 1)
                if c == len(NAT) - 1:
                    dve.wait_ge(nat_out, step_no(n, NB, ready(c)))
                    nc.vector.tensor_tensor(negm[p][:, 4:8], negm[p][:, 4:8], negm[p][:, 8:12],
                                            ALU.min).then_inc(negm_done, 1)

            def row_out(n):
                p = n[1] % 2
                dve.wait_ge(nat_done, step_no(n, NB, NB))
                dve.wait_ge(r_ld[p], n[0] * 32 + stored(n[1] // 2))
                nc.vector.tensor_copy(rrow[p][0:QT, :], bank16((NB - 1) % 2)[0:QT, 0:P])\
                  .then_inc(nat_out, 1)

            def low_part(n, t):
                p = n[1] % 2
                dve.wait_ge(exp_done, step_no(n, QT, ready(t)))
                cols = slice(OFF[t], OFF[t] + SEQ - P * t)
                nc.vector.tensor_tensor(pl[p][:, cols], p32[p][:, cols], ph[p][:, cols], ALU.subtract)\
                  .then_inc(plv_done, 1)

            def normalize(n, half):
                b, h = n[1] % 2, n[0] * 2 + n[1] // 2
                src = ps[:, 6 + half, 0:4 * VW].rearrange("p (i c) -> p i c", c=VW)
                dve.wait_ge(o_out, step_no(n, 2, slot_free(half)))
                dve.wait_ge(ocopy, step_no(n, 2, ready(half)))
                nc.vector.reciprocal(recd[half], src[:, :, 2 * DH:VW].rearrange("p i c -> p (i c)"))\
                  .then_inc(rec_done, 1)
                nc.vector.tensor_tensor(osum[half], src[:, :, 0:DH], osum[half], ALU.add)\
                  .then_inc(o_sum, 1)
                dve.wait_ge(rec_done, step_no(n, 2, half + 1))
                dve.wait_ge(o_sum, step_no(n, 2, half + 1))
                tile = b * QT + 4 * half
                dst = oall[:, tile:tile + 4, bass.ds(h * DH, DH)]
                nc.vector.tensor_tensor(dst, osum[half],
                                        recd[half].rearrange("p (i o) -> p i o", o=1)
                                        .broadcast_to([P, 4, DH]), ALU.mult).then_inc(o_out, 1)

            def b_step(n, first=False, last=False, final=False):
                nxt, prv = (n[0], n[1] + 2), (n[0], n[1] - 1)
                if not first:
                    for t in range(4, QT):
                        low_part(prv, t)
                if not final:
                    row_out((n[0], n[1] + 1))
                for c in range(len(NAT)):
                    if not last:
                        maxima(nxt, c)
                    if not first and c in (7, 10):
                        normalize(prv, c // 10)

            for r in range(2):
                for c in range(len(NAT)):
                    maxima((0, r), c)
                if r == 0:
                    row_out((0, 0))
            b_step((0, 0), first=True)
            b_step((0, 1))
            with dve.Fori(0, STEPS // 4 - 1) as i:
                for r in range(4):
                    b_step((i, 2 + r))
            b_step((0, STEPS - 2), last=True)
            b_step((0, STEPS - 1), last=True, final=True)
            for t in range(4, QT):
                low_part((0, STEPS - 1), t)
            for half in range(2):
                normalize((0, STEPS - 1), half)

            dve.wait_ge(o_out, ready(2 * STEPS - 1))

            def c_out_step(t, p, j):
                dve.wait_ge(c_done, ready(t))
                dve.wait_ge(base_ld[p], j * 16 + 16)
                dve.wait_ge(out_st[p], stored(j))
                nc.vector.scalar_tensor_tensor(outc[p], banks(2 * p, 2), 1.0 / (SX * SW), basec[p],
                                               ALU.mult, ALU.add).then_inc(c_out, 1)

            def c_step(t, p, j, first=False):
                dve.wait_ge(oh_done, ready(t))
                nc.vector.tensor_tensor(ol[p], oall[:, bass.ds(t, 1), :].rearrange("p o n -> p (o n)"),
                                        oh[p], ALU.subtract).then_inc(ol_done, 1)
                dve.wait_ge(ott_done, ready(t))
                nc.vector.tensor_copy(ot[p][:, :, 1, :],
                                      bank16(5 + 2 * p).rearrange("p (k t) -> p k t", k=KT))\
                  .then_inc(otl_out, 1)
                if not first:
                    c_out_step(t - 1, 1 - p, j if p else j - 1)

            tile_loop(dve, c_step)
            c_out_step(NT - 1, 1, NT // 2 - 1)

        @block.tensor
        def _(pe):
            for s in (abs_used, xt_done, qt_done, ott_done, c_done):
                pe.sem_inc(s, RING)
            pe.sem_inc(st_done, STACKS * QT)
            pe.sem_inc(pv_done, 4)

            pe.wait_ge(ones_set, 1)
            pe.wait_ge(w_lo, ready(0))
            for j in range(KT):
                for p in range(2):
                    pe.wait_ge(w_lo, ready(2 * j + p))
                    nc.tensor.matmul(ps[:, 2 + p, :], ones, absw[p], start=(j == 0), stop=(j == KT - 1))\
                      .then_inc(abs_used, 1)
            pe.wait_ge(const_ld, 16 * 4)

            def turn_x(t, p):
                pe.wait_ge(xl_done, ready(t))
                pe.wait_ge(xth_out, slot_free(t))
                pe.wait_ge(xtl_out, slot_free(t))
                for c, part in enumerate((xh[p], xl[p])):
                    for k in range(KT):
                        ins = nc.tensor.transpose(bank16(4 + 2 * p + c)[:, k * P:(k + 1) * P],
                                                  part[:, k * P:(k + 1) * P], idh)
                ins.then_inc(xt_done, 1)

            def product(dst, lhs, wparts, passes):
                order = [(a, b) for a in range(2) for b in range(2) if (a, b) in passes]
                for k in range(KT):
                    for a, b in order:
                        for c in range(2):
                            ins = nc.tensor.matmul(dst[c], lhs(k, a),
                                                   wparts[:, k, b, c * HALF:(c + 1) * HALF],
                                                   start=(k == 0 and (a, b) == order[0]),
                                                   stop=(k == KT - 1 and (a, b) == order[-1]))
                return ins

            THREE = ((0, 0), (0, 1), (1, 0))
            TWO = ((0, 0), (1, 0))

            def block_product(blk, t, p):
                pe.wait_ge(mm_out, slot_free(t + NT * blk))
                product([ps[:, 2 * p + c, :] for c in range(2)],
                        lambda k, a: xnt[:, k, a, bass.ds(t * P, P)],
                        wsl[blk % 2], TWO if blk == F else THREE).then_inc(mm_done, 1)

            def f_step(t, p, j, first=False):
                turn_x(t, p)
                if not first:
                    pe.wait_ge(xth_out, ready(t - 1))
                    pe.wait_ge(xtl_out, ready(t - 1))
                    block_product(F, t - 1, 1 - p)

            pe.wait_ge(alpha_set, 1)
            tile_loop(pe, f_step)
            pe.wait_ge(xth_out, ready(NT - 1))
            pe.wait_ge(xtl_out, ready(NT - 1))
            block_product(F, NT - 1, 1)

            def turn_qk(q, p):
                pe.wait_ge(lo_done, ready(q))
                pe.wait_ge(qt_out, slot_free(q))
                for m in range(HEADS // 2):
                    src = qhl[p][:, 2 * m:2 * m + 2, :, :].rearrange("p h s d -> p (h s d)")
                    ins = nc.tensor.transpose(bank16(4 + 2 * p + m // 8)[:, (m % 8) * P:(m % 8 + 1) * P],
                                              src, idh)
                ins.then_inc(qt_done, 1)

            for blk in (Q, K, V):
                pe.wait_ge(w_lo, ready(NT * (blk + 1) - 1))

                def step(t, p, j, first=False):
                    block_product(blk, t, p)
                    if blk == V and not first or blk == Q and first:
                        return
                    turn_qk(t + (NT * (blk - 1) - 1), 1 - p)

                tile_loop(pe, step)

            def nat(n, c):
                s = n[1] % STACKS
                pe.wait_ge(nat_out, step_no(n, NB, slot_free(c)))
                for i, key, width, col in NAT[c]:
                    dst = ps[:, c % 2, col:col + width]
                    diagonal = key + width == P * (i + 1)
                    ins = nc.tensor.matmul(dst, qs[s][:, i * P:(i + 1) * P], ks[s][:, key:key + width],
                                           start=True, stop=not diagonal)
                    if diagonal:
                        ins = nc.tensor.matmul(dst[:, width - P:width], idb, mnat, start=False, stop=True)
                ins.then_inc(nat_done, 1)

            def row(n):
                pe.wait_ge(negm_done, step_no(n) + 1)
                pe.wait_ge(nat_out, step_no(n, NB, slot_free(NB - 1)))
                nc.tensor.transpose(bank16((NB - 1) % 2)[0:QT, 0:P], negm[n[1] % 2][:, 0:QT], idh)\
                  .then_inc(nat_done, 1)

            def scores(n, t):
                s = n[1] % STACKS
                pe.wait_ge(exp_done, step_no(n, QT, slot_free(t)))
                dst = banks(2 + 2 * (t % 2), 2)
                base = 0 if t < 4 else HALF
                lhs = ks[s][:, t * P:(t + 1) * P]
                for q0 in range(P * t // HALF * HALF, SEQ, HALF):
                    lo = max(q0, P * t)
                    ins = nc.tensor.matmul(dst[:, lo - base:q0 + HALF - base], lhs, qs[s][:, lo:q0 + HALF],
                                           start=True, stop=(lo != P * t))
                    if lo == P * t:
                        ins = nc.tensor.matmul(dst[:, lo - base:lo + P - base], idb, mtr,
                                               start=False, stop=True)
                ins.then_inc(st_done, 1)

            def with_v(n, i):
                p, b, h = n[1] % 2, n[1] % 2, n[0] * 2 + n[1] // 2
                half = i // 4
                if i == 0:
                    pe.wait_ge(plp_done, step_no(n, 4, ready(3)))
                if i >= 4:
                    pe.wait_ge(plv_done, step_no(n, 4, i - 3))
                if i % 4 == 0:
                    pe.wait_ge(o_out, step_no(n, 2, slot_free(half)))
                dst = ps[:, 6 + half, (i % 4) * VW:(i % 4 + 1) * VW]
                for t in range(i + 1):
                    at = OFF[t] + P * (i - t)
                    rhs = vall[:, b * QT + t, bass.ds(h, 1), :].rearrange("p o c -> p (o c)")
                    for part in (ph[p], pl[p]):
                        ins = nc.tensor.matmul(dst, part[:, at:at + P], rhs,
                                               start=(t == 0 and part is ph[p]),
                                               stop=(t == i and part is pl[p]))
                if i % 4 == 3:
                    ins.then_inc(pv_done, 1)

            def head_loaded(n):
                pe.wait_ge(head_ld[n[1] % STACKS], n[0] * (16 * 6) + (n[1] // STACKS + 1) * 16 * 6)

            NAT_AT = {1: (0, 1), 2: (2, 3), 3: (4, 5), 4: (6,), 5: (7, 8), 6: (9,), 7: (10,)}
            PV_AT = {3: (0, 1), 4: (2, 3), 5: (4,), 6: (5, 6), 7: (7,)}

            def b_step(n, first=False, last=False, final=False):
                nxt, prv = (n[0], n[1] + 2), (n[0], n[1] - 1)
                pe.wait_ge(r_ld[n[1] % 2], n[0] * 32 + stored(n[1] // 2 + 1))
                if not last:
                    head_loaded(nxt)
                for t in range(QT):
                    scores(n, t)
                    if t == 0 and not final:
                        row((n[0], n[1] + 1))
                    if not last:
                        for c in NAT_AT.get(t, ()):
                            nat(nxt, c)
                    if not first:
                        for i in PV_AT.get(t, ()):
                            with_v(prv, i)

            pe.wait_ge(extra_ld, 16 * 2 * STACKS)
            pe.wait_ge(mm_out, ready(NT * 4 - 1))
            pe.wait_ge(qt_out, ready(NT * 2 - 1))
            for r in range(2):
                head_loaded((0, r))
                for c in range(len(NAT)):
                    nat((0, r), c)
                if r == 0:
                    row((0, 0))
            pe.wait_ge(v_ld, 16 * 4)
            b_step((0, 0), first=True)
            b_step((0, 1))
            with pe.Fori(0, STEPS // 4 - 1) as i:
                for r in range(4):
                    b_step((i, 2 + r))
            b_step((0, STEPS - 2), last=True)
            b_step((0, STEPS - 1), last=True, final=True)
            for i in range(QT):
                with_v((0, STEPS - 1), i)

            def turn_o(t, p):
                pe.wait_ge(ol_done, ready(t))
                pe.wait_ge(oth_out, slot_free(t))
                pe.wait_ge(otl_out, slot_free(t))
                for c, part in enumerate((oh[p], ol[p])):
                    for k in range(KT):
                        ins = nc.tensor.transpose(bank16(4 + 2 * p + c)[:, k * P:(k + 1) * P],
                                                  part[:, k * P:(k + 1) * P], idh)
                ins.then_inc(ott_done, 1)

            def out_product(t, p):
                pe.wait_ge(oth_out, ready(t))
                pe.wait_ge(otl_out, ready(t))
                pe.wait_ge(c_out, slot_free(t))
                product([ps[:, 2 * p + c, :] for c in range(2)], lambda k, a: ot[p][:, k, a, :],
                        wo, THREE).then_inc(c_done, 1)

            def c_step(t, p, j, first=False):
                turn_o(t, p)
                if not first:
                    out_product(t - 1, 1 - p)

            pe.wait_ge(exp_done, ready(QT * STEPS - 1))
            pe.wait_ge(nat_out, ready(NB * STEPS - 1))
            pe.wait_ge(o_out, ready(2 * STEPS - 1))
            pe.wait_ge(wo_ld, 32)
            tile_loop(pe, c_step)
            out_product(NT - 1, 1)


_INS = ["L0_attn_hidden_states", "L0_attn_Wqkv", "L0_attn_Wout", "L0_ffn_weight_real", "L0_ffn_bias",
        "L0_attn_q_ln_w", "L0_attn_q_ln_b", "L0_attn_k_ln_w", "L0_attn_k_ln_b"]


def _constants():
    import numpy as np

    eye = np.eye(P)
    later = np.arange(P)[None, :] > np.arange(P)[:, None]
    nat = np.where(later, -1e30, 0.0)
    q_extra = np.zeros((DH, SEQ), np.float16)
    q_extra[1:4] = 1.0
    slopes = 1.0 / np.power(2.0, np.arange(1, HEADS + 1, dtype=np.float32) * (8.0 / HEADS))
    rest = slopes[:, None].astype(np.float64) * (np.arange(SEQ) - SEQ // 2)[None, :] * np.sqrt(float(DH))
    k_extra = np.zeros((HEADS, 4, SEQ), np.float16)
    k_extra[:, 0] = 1.0
    for r in range(1, 4):
        k_extra[:, r] = rest.astype(np.float16)
        rest = rest - k_extra[:, r].astype(np.float64)

    def bf(v):
        return (v.astype(np.float32).view(np.uint32) >> 16).astype(np.uint16)

    return {"ident_h": eye.astype(np.float16), "ident_b": bf(eye), "mask_nat": bf(nat),
            "mask_tr": bf(nat.T.copy()), "q_extra": q_extra, "k_extra": k_extra}


def kernel(**inputs):
    import numpy as np
    import concourse.bacc as bacc
    from concourse.bass_utils import run_bass_kernel_spmd

    a = {n: np.ascontiguousarray(inputs[n]) for n in _INS}
    shape = a["L0_attn_hidden_states"].shape
    arrays = {
        "x": a["L0_attn_hidden_states"].reshape(TOK, DM),
        "wqkv_t": np.ascontiguousarray(a["L0_attn_Wqkv"].T),
        "wout_t": np.ascontiguousarray(a["L0_attn_Wout"].T),
        "wffn_t": np.ascontiguousarray(a["L0_ffn_weight_real"].T),
        "ffn_bias": a["L0_ffn_bias"],
        "q_w": a["L0_attn_q_ln_w"], "q_b": a["L0_attn_q_ln_b"],
        "k_w": a["L0_attn_k_ln_w"], "k_b": a["L0_attn_k_ln_b"],
        **_constants(),
    }
    nc = bacc.Bacc("TRN2", target_bir_lowering=False, num_devices=1)
    args = [nc.dram_tensor(f"in_{n}", v.shape, mybir.dt.from_np(v.dtype), kind="ExternalInput").ap()
            for n, v in arrays.items()]
    out = nc.dram_tensor("out_dram", (TOK, DM), F32, kind="ExternalOutput").ap()
    build_program(nc, *args, out)
    r = run_bass_kernel_spmd(nc, [{f"in_{n}": v for n, v in arrays.items()}], core_ids=[0])
    return r.results[0]["out_dram"].reshape(shape)
```

```python
from contextlib import ExitStack

import concourse.bass as bass
from concourse import mybir

F32, F16, BF16, U16 = mybir.dt.float32, mybir.dt.float16, mybir.dt.bfloat16, mybir.dt.uint16
ALU = mybir.AluOpType
ACT = mybir.ActivationFunctionType
AX = mybir.AxisListType.X

P = 128
BATCH, SEQ, DM = 2, 1024, 1024
HEADS, DH = 32, 32
TOK = BATCH * SEQ
NT = TOK // P
KT = DM // P
QT = SEQ // P
HALF = 512
LN_EPS = 1e-5
CLIP = 8.0
SX = 256.0
SW = 256.0
VW = 2 * DH + 1

RING = 2


def ready(n, ring=RING):
    return n + 1 + ring


def slot_free(n):
    return n + 1


def stored(j):
    return 16 * j + 16


def tile_loop(eng, step):
    step(0, 0, 0, first=True)
    with eng.Fori(0, NT // 2 - 1) as it:
        step(it * 2 + 1, 1, it)
        step(it * 2 + 2, 0, it + 1)
    step(NT - 1, 1, NT // 2 - 1)


def staggered_loop(eng, step):
    for t in range(2):
        step(t, t, 0, t)
    with eng.Fori(1, NT // 2 - 1) as it:
        for p in range(2):
            step(it * 2 + p, p, it, None)
    for t in range(NT - 2, NT):
        step(t, t % 2, t // 2, t)


def build_program(nc, x, wqkv_t, wout_t, wffn_t, ffn_bias, q_w, q_b, k_w, k_b,
                  ident_h, ident_b, mask_nat, mask_tr, q_extra, k_extra, out):
    q_scr = nc.dram_tensor("q_scr", [HEADS, 2 * DH, TOK], F16, kind="Internal").ap()
    k_scr = nc.dram_tensor("k_scr", [HEADS, 2 * DH, TOK], F16, kind="Internal").ap()
    raw_scr = nc.dram_tensor("raw_scr", [NT, P, HEADS, VW], F32, kind="Internal").ap()
    v_scr = nc.dram_tensor("v_scr", [NT, P, HEADS * VW], F16, kind="Internal").ap()
    base_scr = nc.dram_tensor("base_scr", [NT, P, DM], F32, kind="Internal").ap()

    ctx = ExitStack()
    with ctx:
        WORDS = 52864
        arena = ctx.enter_context(nc.sbuf_tensor("arena", [P, WORDS], F32))
        small = ctx.enter_context(nc.sbuf_tensor("small", [P, 288], F32))

        def f32(at, n):
            return arena[:, at:at + n]

        def f16(at, n):
            return arena[:, at:at + n // 2].bitcast(F16)

        at = 0
        idh = f16(at, P); at += P // 2
        idb = arena[:, at:at + P // 2].bitcast(BF16); at += P // 2
        mnat = arena[:, at:at + P // 2].bitcast(BF16); at += P // 2
        mtr = arena[:, at:at + P // 2].bitcast(BF16); at += P // 2
        ones = f32(at, P); at += P
        START = at

        at = START
        xnt = f16(at, KT * 2 * TOK).rearrange("p (t k s c) -> p t k s c", t=NT, k=KT, s=2)
        at += KT * TOK
        wsl = [f16(at + s * KT * DM, KT * 2 * DM).rearrange("p (k s n) -> p k s n", k=KT, s=2)
               for s in range(2)]; at += 2 * KT * DM
        wf = [f32(START + KT * TOK + KT * DM + j * DM, DM) for j in range(KT)]
        stage = [f32(at + s * HALF, HALF) for s in range(2)]; at += 2 * HALF
        asum = [f32(at, DM)]; at += DM
        xc = [f32(at + s * DM, DM) for s in range(2)]; at += 2 * DM
        u = [f32(at + s * DM, DM) for s in range(2)]; at += 2 * DM
        split_at = at
        xh = [f16(split_at + s * DM, DM) for s in range(2)]
        xl = [f16(split_at + s * DM + DM // 2, DM) for s in range(2)]
        qhl = [f16(split_at + s * DM, 2 * DM).rearrange("p (h s d) -> p h s d", h=HEADS, s=2)
               for s in range(2)]; at += 2 * DM
        turn_at = at
        fb = [f32(turn_at + s * DM, DM) for s in range(2)]
        asum += [f32(turn_at + 2 * DM, DM)]
        tbuf = [f16(turn_at + s * DM, 2 * DM).rearrange("p (j t) -> p j t", j=HEADS // 2)
                for s in range(2)]; at += 4 * DM
        vst_at = at
        alpha = f32(vst_at, DM)
        vst = [f16(vst_at + s * HEADS * VW // 2, HEADS * VW).rearrange("p (h c) -> p h c", h=HEADS)
               for s in range(2)]; at += HEADS * VW
        ln_at = at
        ln_w = {"q": f32(at, DM), "k": f32(at + DM, DM)}; at += 2 * DM
        ln_b = {"q": f32(at, DM), "k": f32(at + DM, DM)}; at += 2 * DM
        assert at <= WORDS, at

        XNT_AT, W0_AT, W1_AT = START, START + KT * TOK, START + KT * TOK + KT * DM
        VTILE = HEADS * VW // 2
        PCOLS = sum(SEQ - P * t for t in range(QT))
        OFF = [sum(SEQ - P * s for s in range(t)) for t in range(QT)]
        PWORDS = PCOLS + PCOLS // 2
        p_at = [XNT_AT + QT * DM, W1_AT]
        low_at = W1_AT + KT * DM
        v_at = [XNT_AT + t * VTILE for t in range(QT - 1)] + [ln_at + VTILE]
        v_at += [low_at + t * VTILE for t in range(QT - 1)] + [ln_at]
        assert (QT - 1) * VTILE <= QT * DM and PWORDS <= QT * DM and PWORDS <= KT * DM
        assert low_at + (QT - 1) * VTILE <= turn_at
        vtile = [f16(v, HEADS * VW).rearrange("p (h c) -> p h c", h=HEADS) for v in v_at]
        p32 = [f32(v, PCOLS) for v in p_at]
        ph = [v.bitcast(BF16)[:, 1:2 * PCOLS:2] for v in p32]
        pl = [f16(v + PCOLS, PCOLS) for v in p_at]
        STACKS = 4
        qs = [f16(turn_at + s * SEQ // 2, SEQ) for s in range(STACKS)]
        ks = [f16(turn_at + (STACKS + s) * SEQ // 2, SEQ) for s in range(STACKS)]
        raw = [f32(ln_at + 2 * VTILE + s * 4 * VW, 4 * VW) for s in range(2)]
        assert 2 * VTILE + 8 * VW + DM <= 4 * DM

        at = XNT_AT
        rawc = [f32(at + s * HEADS * VW, HEADS * VW).rearrange("p (h c) -> p h c", h=HEADS)
                for s in range(2)]; at += 2 * HEADS * VW
        oc = [f32(at + s * DM, DM) for s in range(2)]; at += 2 * DM
        oh = [f16(at + s * DM, DM) for s in range(2)]
        ol = [f16(at + s * DM + DM // 2, DM) for s in range(2)]; at += 2 * DM
        ot = [f16(at + s * DM, 2 * DM).rearrange("p (k s t) -> p k s t", k=KT, s=2) for s in range(2)]
        at += 2 * DM
        basec = [f32(at + s * DM, DM) for s in range(2)]; at += 2 * DM
        outc = [f32(at + s * DM, DM) for s in range(2)]; at += 2 * DM
        assert at <= W0_AT
        xres = [f32(vst_at + s * DM, DM) for s in range(2)]
        bias = f32(ln_at + 2 * VTILE + 8 * VW, DM)
        wo = wsl[0]

        bst = [small[:, 12 * s:12 * s + 12] for s in range(2)]
        mv = [small[:, 24 + 2 * s:26 + 2 * s] for s in range(2)]
        var_eps = [small[:, 28 + s:29 + s] for s in range(2)]
        rs = [small[:, 30 + s:31 + s] for s in range(2)]
        nb = [small[:, 32 + s:33 + s] for s in range(2)]
        expo, eps_x, eps_qk, plus_sx, minus_sx = (small[:, c:c + 1] for c in range(44, 49))
        plain = [small[:, 49 + s:50 + s] for s in range(2)]
        minus = [small[:, 51 + s:52 + s] for s in range(2)]
        negm = [small[:, 56 + 8 * s:64 + 8 * s].bitcast(F16) for s in range(2)]
        rrow = [small[:, 72 + P // 2 * s:72 + P // 2 * (s + 1)].bitcast(F16) for s in range(2)]
        recc = [small[:, 200 + HEADS * s:200 + HEADS * (s + 1)] for s in range(2)]

        ps = ctx.enter_context(nc.psum_tensor("ps", [P, 8, HALF], F32))

        def banks(b, n):
            return ps[:, b:b + n, :].rearrange("p b n -> p (b n)")

        def bank16(b):
            return ps[:, b, :].bitcast(F16)

        def sem(name):
            return ctx.enter_context(nc.semaphore(name))

        const_ld = sem("const_ld")
        bc_ld = sem("bc_ld")
        bias_ld = sem("bias_ld")
        wf_ld = [sem(f"wf_ld{j}") for j in range(KT)]
        x_ld = [sem(f"x_ld{s}") for s in range(2)]
        w_ld = [sem(f"w_ld{s}") for s in range(2)]
        base_st = [sem(f"base_st{s}") for s in range(2)]
        t_st = [sem(f"t_st{s}") for s in range(2)]
        v_st = [sem(f"v_st{s}") for s in range(2)]
        v_ld = [sem(f"v_ld{b}") for b in range(BATCH)]
        head_ld = [sem(f"head_ld{s}") for s in range(STACKS)]
        extra_ld = sem("extra_ld")
        r_ld = [sem(f"r_ld{s}") for s in range(2)]
        raw_st = [sem(f"raw_st{s}") for s in range(2)]
        raw_ld = [sem(f"raw_ld{s}") for s in range(2)]
        base_ld = [sem(f"base_ld{s}") for s in range(2)]
        out_st = [sem(f"out_st{s}") for s in range(2)]
        setup = sem("setup")
        ones_set = sem("ones_set")
        alpha_set = sem("alpha_set")
        nb_part = sem("nb_part")
        w_hi = sem("w_hi")
        w_lo = sem("w_lo")
        sign_done = sem("sign_done")
        abs_done = sem("abs_done")
        asump_done = sem("asump_done")
        asumv_done = sem("asumv_done")
        alpha_sum = sem("alpha_sum")
        bn_part = sem("bn_part")
        stats = sem("stats")
        ve_done = sem("ve_done")
        pow_done = sem("pow_done")
        rstd_done = sem("rstd_done")
        xn_done = sem("xn_done")
        xh_done = sem("xh_done")
        xl_done = sem("xl_done")
        xt_done = sem("xt_done")
        xth_out = sem("xth_out")
        xtl_out = sem("xtl_out")
        mm_done = sem("mm_done")
        mm_out = sem("mm_out")
        uw_done = sem("uw_done")
        u_done = sem("u_done")
        hi_done = sem("hi_done")
        lo_done = sem("lo_done")
        qt_done = sem("qt_done")
        qt_out = sem("qt_out")
        vh_done = sem("vh_done")
        vl_done = sem("vl_done")
        ones_v = sem("ones_v")
        nat_done = sem("nat_done")
        nat_out = sem("nat_out")
        negm_done = sem("negm_done")
        st_done = sem("st_done")
        exp_done = sem("exp_done")
        plp_done = sem("plp_done")
        plv_done = sem("plv_done")
        pv_done = sem("pv_done")
        raw_out = sem("raw_out")
        xres_done = sem("xres_done")
        resid_done = sem("resid_done")
        recc_done = sem("recc_done")
        osum_done = sem("osum_done")
        o_done = sem("o_done")
        oh_done = sem("oh_done")
        ol_done = sem("ol_done")
        ott_done = sem("ott_done")
        oth_out = sem("oth_out")
        otl_out = sem("otl_out")
        c_done = sem("c_done")
        c_out = sem("c_out")

        w_src = [None, wqkv_t[:, 0:DM], wqkv_t[:, DM:2 * DM], wqkv_t[:, 2 * DM:3 * DM], wout_t]
        F, Q, K, V, WO = range(5)
        LNQ = {Q: "q", K: "k"}
        STEPS = 2 * HEADS
        NAT = [[(0, 0, P, 0), (1, 0, 2 * P, P)], [(2, 0, 3 * P, 0)], [(3, 0, 4 * P, 0)]]
        for i in range(4, QT):
            NAT += [[(i, 0, HALF, 0)], [(i, HALF, P * (i + 1) - HALF, 0)]]
        NB = len(NAT) + 1
        SC = []
        for t in range(QT):
            SC += [(t, max(q0, P * t), q0 + HALF - max(q0, P * t))
                   for q0 in range(P * t // HALF * HALF, SEQ, HALF)]
        NS = len(SC)
        LAST_SC = [max(c for c, x in enumerate(SC) if x[0] == t) for t in range(QT)]
        RB = 3
        NATB, SCB, PVB = (4, 5, 6), (7, 0, 1), (2, 3)
        assert NB % RB == 0 and NS % RB == 0
        POOL_T, DVE_T = (0, 1, 2, 4), (3, 5, 6, 7)
        POOL_END, DVE_END = (0, 3), (1, 2, 4, 5, 6, 7)
        SCALE = float(DH) ** -0.5

        ROW_AT = 5

        def nat_item(n, c):
            return c if n[1] == 0 else c - 1 + (c >= ROW_AT)

        def row_item(n):
            return NB - 1 if n[1] == STEPS - 1 else NB + ROW_AT - 1

        def step_no(n, per_step=1, more=0):
            return n[0] * (4 * per_step) + (n[1] * per_step + more)

        block = ctx.enter_context(nc.Block())

        @block.sync
        def _(sp):
            def load_x(t, p, j):
                sp.wait_ge(xn_done, slot_free(t))
                sp.dma_start(xc[p], x[bass.ds(t * P, P), :]).then_inc(x_ld[p], 16)

            def load_w(blk, t, p, j):
                sp.wait_ge(w_hi, slot_free(t + NT * (blk - 1)))
                sp.wait_ge(w_lo, slot_free(t + NT * (blk - 1)))
                sp.dma_start(stage[p], w_src[blk][bass.ds(j * P, P), p * HALF:(p + 1) * HALF])\
                  .then_inc(w_ld[p], 16)

            def store_base(t, p):
                sp.wait_ge(mm_out, ready(t))
                sp.dma_start(base_scr[bass.ds(t, 1), :, :].rearrange("o p n -> p (o n)"), fb[p])\
                  .then_inc(base_st[p], 16)

            for t in range(2):
                load_x(t, t, 0)
            for dst, src in ((idh, ident_h), (idb.bitcast(U16), ident_b), (mnat.bitcast(U16), mask_nat),
                             (mtr.bitcast(U16), mask_tr)):
                sp.dma_start(dst, src).then_inc(const_ld, 16)
            for j in range(KT):
                sp.dma_start(wf[j], wffn_t[j * P:(j + 1) * P, :]).then_inc(wf_ld[j], 16)
                if j == KT // 2 - 1:
                    load_x(2, 0, 1)
            for t in range(2):
                load_w(Q, t, t, 0)
            for dst, src in ((ln_w["q"], q_w), (ln_b["q"], q_b), (ln_w["k"], k_w), (ln_b["k"], k_b)):
                sp.dma_start(dst, src.partition_broadcast(P)).then_inc(bc_ld, 16)

            load_w(Q, 2, 0, 1)
            load_x(3, 1, 1)
            with sp.Fori(1, NT // 2 - 1) as j:
                load_w(Q, j * 2 + 1, 1, j)
                load_x(j * 2 + 2, 0, j + 1)
                store_base(j * 2 - 2, 0)
                load_w(Q, j * 2 + 2, 0, j + 1)
                load_x(j * 2 + 3, 1, j + 1)
                store_base(j * 2 - 1, 1)
            load_w(Q, NT - 1, 1, NT // 2 - 1)
            for t in range(NT - 4, NT):
                store_base(t, t % 2)
            for blk in (K, V):
                with sp.Fori(0, NT // 2) as j:
                    for p in range(2):
                        load_w(blk, j * 2 + p, p, j)

            def store_v(t, p):
                sp.wait_ge(vl_done, ready(t))
                sp.dma_start(v_scr[bass.ds(t, 1), :, :].rearrange("o p n -> p (o n)"),
                             vst[p].rearrange("p h c -> p (h c)")).then_inc(v_st[p], 16)

            def load_head(n):
                s, b, h = n[1] % STACKS, n[1] % 2, n[0] * 2 + n[1] // 2
                toks = slice(b * SEQ, (b + 1) * SEQ)
                sp.wait_ge(st_done, step_no(n, NS, NS))
                hq = q_scr[bass.ds(h, 1), :, toks].rearrange("o r t -> (o r) t")
                hk = k_scr[bass.ds(h, 1), :, toks].rearrange("o r t -> (o r) t")
                ex = k_extra[bass.ds(h, 1), :, :].rearrange("o r t -> (o r) t")
                sp.dma_start(ks[s][DH:2 * DH], hk[0:DH]).then_inc(head_ld[s], 16)
                sp.dma_start(ks[s][2 * DH:4 * DH], hk).then_inc(head_ld[s], 16)
                sp.dma_start(ks[s][0:4], ex).then_inc(head_ld[s], 16)
                sp.dma_start(qs[s][DH:3 * DH], hq).then_inc(head_ld[s], 16)
                sp.dma_start(qs[s][3 * DH:4 * DH], hq[0:DH]).then_inc(head_ld[s], 16)
                sp.dma_start(qs[s][0:1], q_extra[0:1]).then_inc(head_ld[s], 16)

            def load_row(n):
                sp.wait_ge(nat_out, step_no(n, NB, ready(row_item(n), RB)))
                sp.dma_start(qs[n[1] % STACKS][0:1, :], rrow[n[1] % 2][0:QT, :])\
                  .then_inc(r_ld[n[1] % 2], 16)

            def store_raw(n, half):
                b, h = n[1] % 2, n[0] * 2 + n[1] // 2
                tile = b * QT + 4 * half
                sp.wait_ge(raw_out, step_no(n, 2, ready(half)))
                sp.dma_start(raw_scr[tile:tile + 4, :, bass.ds(h, 1), :]
                             .rearrange("i p o c -> p i (o c)"),
                             raw[half].rearrange("p (i c) -> p i c", c=VW)).then_inc(raw_st[half], 16)

            def load_v(t, n):
                sp.dma_start(f16(v_at[t], n * HEADS * VW).rearrange("p (t c) -> p t c", t=n),
                             v_scr[t:t + n].rearrange("t p c -> p t c")).then_inc(v_ld[t // QT], 16)

            for t in range(2):
                load_w(WO, t, t, 0)
            for s in range(2):
                sp.wait_ge(t_st[s], stored(NT))
            for s in range(STACKS):
                sp.dma_start(ks[s][0:DH], q_extra).then_inc(extra_ld, 16)
                sp.dma_start(qs[s][0:DH], q_extra).then_inc(extra_ld, 16)
            sp.wait_ge(extra_ld, 16 * 2 * STACKS)
            for r in range(STACKS):
                load_head((0, r))
            store_v(0, 0)
            with sp.Fori(1, QT // 2 + 1) as j:
                for p in range(2):
                    load_w(WO, j * 2 + p, p, j)
                    store_v(j * 2 + p - 1, 1 - p)
            sp.wait_ge(mm_done, NT * V + QT)
            for s in range(2):
                sp.wait_ge(v_st[s], stored(QT // 2))
            load_v(0, 4)
            load_v(4, 3)
            load_v(QT - 1, 1)
            with sp.Fori(QT // 2 + 1, NT // 2) as j:
                for p in range(2):
                    load_w(WO, j * 2 + p, p, j)
                    store_v(j * 2 + p - 1, 1 - p)
            load_row((0, 0))
            store_v(NT - 1, 1)
            load_row((0, 1))
            sp.wait_ge(w_lo, ready(NT * 4 - 1))
            sp.wait_ge(vl_done, ready(NT - 1))
            for s in range(2):
                sp.wait_ge(v_st[s], stored(NT // 2))
            load_v(QT, 4)
            load_v(QT + 4, 3)
            load_v(NT - 1, 1)

            def four_steps(i):
                for r in range(4):
                    load_head((i, 4 + r))
                    load_row((i, 2 + r))
                    for half in range(2):
                        store_raw((i, r), half)

            with sp.Fori(0, STEPS // 4 - 1) as i:
                four_steps(i)
            for n in range(STEPS - 4, STEPS - 1):
                if n < STEPS - 2:
                    load_row((0, n + 2))
                for half in range(2):
                    store_raw((0, n), half)

            def load_tile(t, p):
                sp.wait_ge(osum_done, slot_free(t))
                sp.wait_ge(recc_done, slot_free(t))
                sp.dma_start(rawc[p].rearrange("p h c -> p (h c)"),
                             raw_scr[bass.ds(t, 1), :, :, :].rearrange("o p h c -> p (o h c)"))\
                  .then_inc(raw_ld[p], 16)

            def load_base(t, p):
                sp.wait_ge(c_out, slot_free(t))
                sp.dma_start(basec[p], base_scr[bass.ds(t, 1), :, :].rearrange("o p n -> p (o n)"))\
                  .then_inc(base_ld[p], 16)
                sp.dma_start(xres[p], x[bass.ds(t * P, P), :]).then_inc(base_ld[p], 16)

            def store_out(t, p):
                sp.wait_ge(c_out, ready(t))
                sp.dma_start(out[bass.ds(t * P, P), :], outc[p]).then_inc(out_st[p], 16)

            sp.wait_ge(pv_done, 2 * (STEPS - 1) + 4)
            for half in range(2):
                sp.wait_ge(raw_st[half], stored(STEPS - 1))
            for t in range(2):
                load_tile(t, t)
            sp.dma_start(bias, ffn_bias.partition_broadcast(P)).then_inc(bias_ld, 16)
            for half in range(2):
                store_raw((0, STEPS - 1), half)
            for t in range(2):
                load_base(t, t)
            for half in range(2):
                sp.wait_ge(raw_st[half], stored(STEPS))

            def c_step(t, p, last=False):
                if not last:
                    load_tile(t + 1, 1 - p)
                load_base(t, p)
                store_out(t - 2, p)

            load_tile(2, 0)
            with sp.Fori(1, NT // 2 - 1) as j:
                for p in range(2):
                    c_step(j * 2 + p, p)
            c_step(NT - 2, 0)
            c_step(NT - 1, 1, last=True)
            for p in range(2):
                store_out(NT - 2 + p, p)
            for p in range(2):
                sp.wait_ge(out_st[p], stored(NT // 2))

        @block.gpsimd
        def _(pool):
            for s in (rstd_done, lo_done, o_done, resid_done):
                pool.sem_inc(s, RING)
            for col, value in ((expo, -0.5), (eps_x, LN_EPS), (eps_qk, LN_EPS * (SX * SW) ** 2),
                               (plus_sx, SX), (minus_sx, -SX)):
                nc.gpsimd.memset(col, value).then_inc(setup, 1)
            pool.wait_ge(setup, 5)

            def variance_plus(g, p, eps):
                pool.wait_ge(stats, ready(g))
                nc.gpsimd.tensor_tensor(var_eps[p], mv[p][:, 1:2], eps, ALU.add).then_inc(ve_done, 1)
                pool.wait_ge(ve_done, g + 1)

            def f_step(t, p):
                variance_plus(t, p, eps_x)
                nc.gpsimd.tensor_tensor(plain[p], var_eps[p], expo, ALU.pow).then_inc(pow_done, 1)
                pool.wait_ge(pow_done, t + 1)
                pool.wait_ge(xn_done, slot_free(t))
                nc.gpsimd.tensor_tensor(minus[p], plain[p], minus_sx, ALU.mult)
                nc.gpsimd.tensor_tensor(rs[p], plain[p], plus_sx, ALU.mult).then_inc(nb_part, 1)
                pool.wait_ge(nb_part, t + 1)
                nc.gpsimd.tensor_tensor(nb[p], mv[p][:, 0:1], minus[p], ALU.mult).then_inc(rstd_done, 1)

            for t in range(2):
                f_step(t, t)
            for j in range(1, KT // 2):
                pool.wait_ge(abs_done, j + 1)
                if j > 1:
                    pool.wait_ge(asump_done, j - 1)
                nc.gpsimd.tensor_tensor(asum[0], wf[0] if j == 1 else asum[0], wf[j], ALU.add)\
                  .then_inc(asump_done, 1)
            with pool.Fori(1, NT // 2) as i:
                for p in range(2):
                    f_step(i * 2 + p, p)

            for blk in (Q, K):
                def qk_step(t, p, j, first=False):
                    g, q = t + NT * blk, t + NT * (blk - 1)
                    variance_plus(g, p, eps_qk)
                    pool.wait_ge(u_done, slot_free(q))
                    nc.gpsimd.tensor_tensor(rs[p], var_eps[p], expo, ALU.pow).then_inc(rstd_done, 1)
                    pool.wait_ge(hi_done, ready(q))
                    nc.gpsimd.tensor_tensor(qhl[p][:, :, 1, :],
                                            u[p].rearrange("p (h d) -> p h d", h=HEADS),
                                            qhl[p][:, :, 0, :], ALU.subtract).then_inc(lo_done, 1)

                tile_loop(pool, qk_step)

            for s in range(2):
                pool.wait_ge(base_st[s], stored(NT // 2))
            for s in range(2):
                nc.gpsimd.memset(vst[s][:, :, 2 * DH:VW], 1.0).then_inc(ones_v, 1)

            def low_parts(n):
                p = n[1] % 2
                for t in POOL_END if n[1] >= STEPS - 2 else POOL_T:
                    pool.wait_ge(exp_done, step_no(n, NS, ready(LAST_SC[t], RB)))
                    cols = slice(OFF[t], OFF[t] + SEQ - P * t)
                    nc.gpsimd.tensor_tensor(pl[p][:, cols], p32[p][:, cols], ph[p][:, cols],
                                            ALU.subtract).then_inc(plp_done, 1)

            with pool.Fori(0, STEPS // 4 - 1) as i:
                for r in range(4):
                    low_parts((i, r))
            for n in range(STEPS - 4, STEPS):
                low_parts((0, n))

            def residual(t, p, j):
                pool.wait_ge(bias_ld, 16)
                pool.wait_ge(base_ld[p], j * 32 + 32)
                nc.gpsimd.tensor_tensor(basec[p], basec[p], xres[p], ALU.add).then_inc(xres_done, 1)
                pool.wait_ge(xres_done, t + 1)
                nc.gpsimd.tensor_tensor(basec[p], basec[p], bias, ALU.add).then_inc(resid_done, 1)

            def c_step(t, p, j, first=False):
                pool.wait_ge(osum_done, ready(t))
                pool.wait_ge(recc_done, ready(t))
                o = oc[p].rearrange("p (h d) -> p h d", h=HEADS)
                nc.gpsimd.tensor_tensor(o, o, recc[p].rearrange("p (h o) -> p h o", o=1)
                                        .broadcast_to([P, HEADS, DH]), ALU.mult).then_inc(o_done, 1)
                if not first:
                    residual(t - 1, 1 - p, j if p else j - 1)

            tile_loop(pool, c_step)
            residual(NT - 1, 1, NT // 2 - 1)

        @block.scalar
        def _(act):
            for s in (w_hi, xn_done, xh_done, xth_out, hi_done, qt_out, vh_done, raw_out,
                      oh_done, oth_out):
                act.sem_inc(s, RING)
            act.sem_inc(exp_done, RB)
            for s in (*t_st, *v_st, *raw_st):
                act.sem_inc(s, 16)

            def split_hi(blk, t, p, j):
                act.wait_ge(w_ld[p], j * 16 + (16 * KT * (blk - 1) + 16))
                nc.scalar.activation(wsl[blk % 2][:, bass.ds(j, 1), 0, p * HALF:(p + 1) * HALF]
                                     .rearrange("p o n -> p (o n)"), stage[p], ACT.Copy, scale=SW)\
                  .then_inc(w_hi, 1)

            def xt_high(t, p):
                act.wait_ge(xt_done, ready(t))
                nc.scalar.activation(xnt[:, bass.ds(t, 1), :, 0, :].rearrange("p o k c -> p (o k) c"),
                                     bank16(4 + 2 * p).rearrange("p (k t) -> p k t", k=KT), ACT.Copy)\
                  .then_inc(xth_out, 1)

            def normalize_x(t, p, j):
                act.wait_ge(x_ld[p], j * 16 + 16)
                act.wait_ge(rstd_done, ready(t))
                act.wait_ge(xl_done, slot_free(t))
                nc.scalar.activation(u[p], xc[p], ACT.Identity, bias=nb[p], scale=rs[p])\
                  .then_inc(xn_done, 1)
                act.wait_ge(xn_done, ready(t))
                act.wait_ge(xt_done, slot_free(t))
                nc.scalar.activation(xh[p], u[p], ACT.Copy).then_inc(xh_done, 1)

            for t in range(2):
                normalize_x(t, t, 0)
            for j in range(KT):
                act.wait_ge(wf_ld[j], 16)
                nc.scalar.activation(wsl[F][:, j, 0, :], wf[j], ACT.Sign).then_inc(sign_done, 1)
            xt_high(0, 0)
            act.wait_ge(asump_done, KT // 2 - 1)
            act.wait_ge(asumv_done, KT // 2 - 1)
            for t in range(2):
                split_hi(Q, t, t, 0)
            with act.Fori(1, NT // 2) as j:
                for p in range(2):
                    xt_high(j * 2 + p - 1, 1 - p)
                    split_hi(Q, j * 2 + p, p, j)
                    normalize_x(j * 2 + p, p, j)
            xt_high(NT - 1, 1)

            def turn_out(scr, q, t, p, stores):
                act.wait_ge(qt_done, ready(q))
                act.wait_ge(t_st[p], stored(stores))
                half = HEADS // 4
                for c in range(2):
                    ins = nc.scalar.activation(
                        tbuf[p][:, c * half:(c + 1) * half, :],
                        bank16(4 + 2 * p + c).rearrange("p (j t) -> p j t", t=P), ACT.Copy)
                ins.then_inc(qt_out, 1)
                act.wait_ge(qt_out, ready(q))
                dst = scr.rearrange("h r t -> (h r) t").rearrange("(j p) t -> p j t", p=P)
                act.dma_start(dst[:, :, bass.ds(t * P, P)], tbuf[p]).then_inc(t_st[p], 16)

            for s in range(2):
                act.wait_ge(base_st[s], stored(NT // 2))

            for blk in (Q, K):
                act.wait_ge(mm_done, NT * blk)

                def qk_step(t, p, j, first=False):
                    q = t + NT * (blk - 1)
                    split_hi(blk + 1, t, p, j)
                    if not first:
                        before = (j if p else j - 1) + NT // 2 * (blk - 1)
                        turn_out({Q: q_scr, K: k_scr}[blk], q - 1, t - 1, 1 - p, before)
                    elif blk == K:
                        turn_out(q_scr, NT - 1, NT - 1, 1, NT // 2 - 1)
                    act.wait_ge(u_done, ready(q))
                    act.wait_ge(qt_done, slot_free(q))
                    nc.scalar.activation(qhl[p][:, :, 0, :],
                                         u[p].rearrange("p (h d) -> p h d", h=HEADS),
                                         ACT.Copy).then_inc(hi_done, 1)

                tile_loop(act, qk_step)

            act.wait_ge(mm_done, NT * V)
            act.wait_ge(ones_v, 2)

            def v_step(t, p, j, first=False):
                split_hi(WO, t, p, j)
                if first:
                    turn_out(k_scr, 2 * NT - 1, NT - 1, 1, NT - 1)
                act.wait_ge(mm_out, ready(t + NT * V))
                act.wait_ge(v_st[p], stored(j))
                nc.scalar.activation(vst[p][:, :, 0:DH], xc[p].rearrange("p (h d) -> p h d", h=HEADS),
                                     ACT.Copy, scale=1.0 / SW).then_inc(vh_done, 1)

            tile_loop(act, v_step)

            def exps(n, c):
                p = n[1] % 2
                t, q0, w = SC[c]
                act.wait_ge(st_done, step_no(n, NS, c + 1 + STACKS * NS))
                if c == 0:
                    act.wait_ge(pv_done, step_no(n, 2, 2))
                at = OFF[t] + q0 - P * t
                nc.scalar.activation(p32[p][:, at:at + w], ps[:, SCB[c % RB], q0 % HALF:q0 % HALF + w],
                                     ACT.Exp, scale=SCALE).then_inc(exp_done, 1)

            def raw_copy(n, half):
                act.wait_ge(pv_done, step_no(n, 2, half + 5))
                act.wait_ge(raw_st[half], step_no(n, 16, 16))
                nc.scalar.activation(raw[half], ps[:, PVB[half], 0:4 * VW], ACT.Copy)\
                  .then_inc(raw_out, 1)

            RAW_AFTER = {6: 0, 11: 1}

            def b_step(n, first=False):
                for c in range(NS):
                    exps(n, c)
                    if c in RAW_AFTER and not first:
                        raw_copy((n[0], n[1] - 1), RAW_AFTER[c])

            act.wait_ge(mm_done, NT * 4)
            b_step((0, 0), first=True)
            b_step((0, 1))
            with act.Fori(0, STEPS // 4 - 1) as i:
                for r in range(4):
                    b_step((i, 2 + r))
            b_step((0, STEPS - 2))
            b_step((0, STEPS - 1))
            for half in range(2):
                raw_copy((0, STEPS - 1), half)

            def ot_high(t, p):
                act.wait_ge(ott_done, ready(t))
                act.wait_ge(c_done, slot_free(t))
                nc.scalar.activation(ot[p][:, :, 0, :],
                                     bank16(4 + 2 * p).rearrange("p (k t) -> p k t", k=KT),
                                     ACT.Copy).then_inc(oth_out, 1)

            def c_step(t, p, j, edge):
                if edge != 0:
                    ot_high(t - 1, 1 - p)
                act.wait_ge(o_done, ready(t))
                act.wait_ge(ott_done, slot_free(t))
                nc.scalar.activation(oh[p], oc[p], ACT.Copy).then_inc(oh_done, 1)

            staggered_loop(act, c_step)
            ot_high(NT - 1, 1)

        @block.vector
        def _(dve):
            for s in (w_lo, stats, xl_done, xtl_out, mm_out, u_done, vl_done,
                      recc_done, osum_done, ol_done, otl_out, c_out):
                dve.sem_inc(s, RING)
            dve.sem_inc(nat_out, RB)
            for s in (*base_st, *out_st, *r_ld):
                dve.sem_inc(s, 16)
            nc.vector.memset(ones, 1.0).then_inc(ones_set, 1)

            def split_lo(blk, t, p, j):
                dve.wait_ge(w_hi, ready(t + NT * (blk - 1)))
                part = [wsl[blk % 2][:, bass.ds(j, 1), s, p * HALF:(p + 1) * HALF]
                        .rearrange("p o n -> p (o n)") for s in range(2)]
                nc.vector.scalar_tensor_tensor(part[1], stage[p], SW, part[0], ALU.mult, ALU.subtract)\
                  .then_inc(w_lo, 1)

            def statistics(g, p, between):
                for c in range(2):
                    ins = nc.vector.bn_stats(bst[p][:, 6 * c:6 * c + 6], xc[p][:, c * HALF:(c + 1) * HALF])
                ins.then_inc(bn_part, 1)
                dve.wait_ge(bn_part, g + 1)
                dve.wait_ge(rstd_done, slot_free(g))
                between()
                nc.vector.bn_aggr(mv[p], bst[p]).then_inc(stats, 1)

            def f_out(t, p, j):
                dve.wait_ge(mm_done, t + 1)
                dve.wait_ge(base_st[p], stored(j))
                nc.vector.tensor_tensor(fb[p], banks(2 * p, 2), alpha, ALU.mult).then_inc(mm_out, 1)

            def xt_low(t, p):
                dve.wait_ge(xt_done, ready(t))
                nc.vector.tensor_copy(xnt[:, bass.ds(t, 1), :, 1, :].rearrange("p o k c -> p (o k) c"),
                                      bank16(5 + 2 * p).rearrange("p (k t) -> p k t", k=KT))\
                  .then_inc(xtl_out, 1)

            def x_low(t, p):
                dve.wait_ge(xh_done, ready(t))
                nc.vector.tensor_tensor(xl[p], u[p], xh[p], ALU.subtract).then_inc(xl_done, 1)

            def f_step(t, p, j, last=False):
                xt_low(t - 1, 1 - p)
                if last:
                    split_lo(Q, t, p, j)
                else:
                    dve.wait_ge(x_ld[1 - p], (j + p) * 16 + 16)
                    statistics(t + 1, 1 - p, lambda: split_lo(Q, t, p, j))
                x_low(t, p)
                f_out(t - 2, p, j - 1)

            for t in range(2):
                dve.wait_ge(x_ld[t], 16)
                statistics(t, t, lambda: None)
            for t in range(2):
                x_low(t, t)
            xt_low(0, 0)
            for j in range(KT):
                dve.wait_ge(sign_done, j + 1)
                nc.vector.scalar_tensor_tensor(wf[j], wf[j], -1.0, wf[j], ALU.mult, ALU.max)\
                  .then_inc(abs_done, 1)
                if j == KT // 2:
                    dve.wait_ge(x_ld[0], 32)
                    statistics(2, 0, lambda: None)
            for j in range(KT // 2 + 1, KT):
                dve.wait_ge(abs_done, j + 1)
                if j > KT // 2 + 1:
                    dve.wait_ge(asumv_done, j - KT // 2 - 1)
                nc.vector.tensor_tensor(asum[1], wf[KT // 2] if j == KT // 2 + 1 else asum[1], wf[j],
                                        ALU.add).then_inc(asumv_done, 1)
            for t in range(2):
                split_lo(Q, t, t, 0)
            dve.wait_ge(alpha_sum, 1)
            nc.vector.tensor_scalar(alpha, banks(2, 2), 1.0 / (DM * SX), None, ALU.mult)\
              .then_inc(alpha_set, 1)
            dve.wait_ge(alpha_set, 1)
            with dve.Fori(1, NT // 2 - 1) as j:
                for p in range(2):
                    f_step(j * 2 + p, p, j)
            f_step(NT - 2, 0, NT // 2 - 1)
            f_step(NT - 1, 1, NT // 2 - 1, last=True)
            xt_low(NT - 1, 1)
            for p in range(2):
                f_out(NT - 2 + p, p, NT // 2 - 1)

            def clipped(g, p):
                dve.wait_ge(mm_done, g + 1)
                lim = CLIP * SX * SW
                nc.vector.tensor_scalar(xc[p], banks(2 * p, 2), lim, -lim, ALU.min, ALU.max)\
                  .then_inc(mm_out, 1)

            dve.wait_ge(xn_done, ready(NT - 1))
            dve.wait_ge(bc_ld, 16 * 4)
            for blk in (Q, K):
                def qk_step(t, p, j, first=False):
                    g, q = t + NT * blk, t + NT * (blk - 1)
                    w, b = ln_w[LNQ[blk]], ln_b[LNQ[blk]]
                    clipped(g, p)
                    dve.wait_ge(mm_out, ready(g))
                    statistics(g, p, lambda: split_lo(blk + 1, t, p, j))
                    dve.wait_ge(rstd_done, ready(g))
                    dve.wait_ge(lo_done, slot_free(q))
                    nc.vector.scalar_tensor_tensor(u[p], xc[p], mv[p][:, 0:1], w, ALU.subtract, ALU.mult)\
                      .then_inc(uw_done, 1)
                    dve.wait_ge(uw_done, q + 1)
                    nc.vector.scalar_tensor_tensor(u[p], u[p], rs[p], b, ALU.mult, ALU.add)\
                      .then_inc(u_done, 1)

                tile_loop(dve, qk_step)

            def maxima(n, c):
                p = n[1] % 2
                dve.wait_ge(nat_done, step_no(n, NB, nat_item(n, c) + 1))
                for i, key, width, col in NAT[c]:
                    at = i if key == 0 else i + 4
                    ins = nc.vector.tensor_reduce(negm[p][:, at:at + 1],
                                                  ps[:, NATB[nat_item(n, c) % RB], col:col + width],
                                                  AX, ALU.max, negate=True)
                ins.then_inc(nat_out, 1)

            def both_halves(n):
                p = n[1] % 2
                dve.wait_ge(nat_out, step_no(n, NB, ready(nat_item(n, len(NAT) - 1), RB)))
                nc.vector.tensor_tensor(negm[p][:, 4:8], negm[p][:, 4:8], negm[p][:, 8:12],
                                        ALU.min).then_inc(negm_done, 1)

            def row_out(n):
                p = n[1] % 2
                dve.wait_ge(nat_done, step_no(n, NB, row_item(n) + 1))
                dve.wait_ge(r_ld[p], n[0] * 32 + stored(n[1] // 2))
                nc.vector.tensor_copy(rrow[p][0:QT, :], bank16(NATB[row_item(n) % RB])[0:QT, 0:P])\
                  .then_inc(nat_out, 1)

            def v_step(t, p, j, edge):
                if edge == NT - 2:
                    for c in range(len(NAT)):
                        maxima((0, 0), c)
                    both_halves((0, 0))
                if edge == NT - 1:
                    for c in range(len(NAT)):
                        if c == ROW_AT:
                            row_out((0, 0))
                        maxima((0, 1), c)
                dve.wait_ge(vh_done, slot_free(t))
                clipped(t + NT * V, p)
                split_lo(WO, t, p, j)
                dve.wait_ge(vh_done, ready(t))
                nc.vector.scalar_tensor_tensor(vst[p][:, :, DH:2 * DH],
                                               xc[p].rearrange("p (h d) -> p h d", h=HEADS),
                                               1.0 / SW, vst[p][:, :, 0:DH], ALU.mult, ALU.subtract)\
                  .then_inc(vl_done, 1)

            staggered_loop(dve, v_step)

            def low_part(n, t):
                p = n[1] % 2
                dve.wait_ge(exp_done, step_no(n, NS, ready(LAST_SC[t], RB)))
                cols = slice(OFF[t], OFF[t] + SEQ - P * t)
                nc.vector.tensor_tensor(pl[p][:, cols], p32[p][:, cols], ph[p][:, cols], ALU.subtract)\
                  .then_inc(plv_done, 1)

            LOW_BEFORE = {5: 5, 6: 6, 7: 7}
            LOW_AFTER = 9

            def b_step(n, first=False, last=False, final=False):
                for c in range(len(NAT)):
                    if c in LOW_BEFORE and not first and not final:
                        low_part((n[0], n[1] - 1), LOW_BEFORE[c])
                    if c == ROW_AT and not final:
                        row_out((n[0], n[1] + 1))
                    if not last:
                        maxima((n[0], n[1] + 2), c)
                    if c == 0 and not final:
                        both_halves((n[0], n[1] + 1))
                    if c == LOW_AFTER and not last:
                        low_part(n, DVE_T[0])
                if last:
                    for t in DVE_END:
                        low_part(n, t)

            b_step((0, 0), first=True)
            b_step((0, 1))
            with dve.Fori(0, STEPS // 4 - 1) as i:
                for r in range(4):
                    b_step((i, 2 + r))
            b_step((0, STEPS - 2), last=True)
            b_step((0, STEPS - 1), last=True, final=True)

            def sums(t, p, j):
                dve.wait_ge(raw_ld[p], j * 16 + 16)
                dve.wait_ge(o_done, slot_free(t))
                nc.vector.reciprocal(recc[p], rawc[p][:, :, 2 * DH:VW].rearrange("p h c -> p (h c)"))\
                  .then_inc(recc_done, 1)
                dve.wait_ge(ol_done, slot_free(t))
                nc.vector.tensor_tensor(oc[p].rearrange("p (h d) -> p h d", h=HEADS),
                                        rawc[p][:, :, 0:DH], rawc[p][:, :, DH:2 * DH], ALU.add)\
                  .then_inc(osum_done, 1)

            def c_out_step(t, p, j):
                dve.wait_ge(c_done, ready(t))
                dve.wait_ge(resid_done, ready(t))
                dve.wait_ge(out_st[p], stored(j))
                nc.vector.scalar_tensor_tensor(outc[p], banks(2 * p, 2), 1.0 / (SX * SW), basec[p],
                                               ALU.mult, ALU.add).then_inc(c_out, 1)

            def ot_low(t, p):
                dve.wait_ge(ott_done, ready(t))
                dve.wait_ge(c_done, slot_free(t))
                nc.vector.tensor_copy(ot[p][:, :, 1, :],
                                      bank16(5 + 2 * p).rearrange("p (k t) -> p k t", k=KT))\
                  .then_inc(otl_out, 1)

            def c_step(t, p, j, edge):
                if edge != 0:
                    ot_low(t - 1, 1 - p)
                dve.wait_ge(oh_done, ready(t))
                nc.vector.tensor_tensor(ol[p], oc[p], oh[p], ALU.subtract).then_inc(ol_done, 1)
                if edge not in (0, 1):
                    c_out_step(t - 2, p, j - 1)
                if edge != NT - 1:
                    sums(t + 1, 1 - p, j + p)

            sums(0, 0, 0)
            staggered_loop(dve, c_step)
            ot_low(NT - 1, 1)
            for p in range(2):
                c_out_step(NT - 2 + p, p, NT // 2 - 1)

        @block.tensor
        def _(pe):
            for s in (xt_done, qt_done, ott_done, c_done):
                pe.sem_inc(s, RING)
            pe.sem_inc(st_done, STACKS * NS)
            pe.sem_inc(pv_done, 4)

            pe.wait_ge(const_ld, 16 * 4)

            def turn_x(t, p):
                pe.wait_ge(xl_done, ready(t))
                pe.wait_ge(xth_out, slot_free(t))
                pe.wait_ge(xtl_out, slot_free(t))
                for c, part in enumerate((xh[p], xl[p])):
                    for k in range(KT):
                        ins = nc.tensor.transpose(bank16(4 + 2 * p + c)[:, k * P:(k + 1) * P],
                                                  part[:, k * P:(k + 1) * P], idh)
                ins.then_inc(xt_done, 1)

            def product(dst, lhs, wparts, passes, between=None):
                order = [(a, b) for a in range(2) for b in range(2) if (a, b) in passes]
                for k in range(KT):
                    for a, b in order:
                        for c in range(2):
                            ins = nc.tensor.matmul(dst[c], lhs(k, a),
                                                   wparts[:, k, b, c * HALF:(c + 1) * HALF],
                                                   start=(k == 0 and (a, b) == order[0]),
                                                   stop=(k == KT - 1 and (a, b) == order[-1]))
                    if between and k < KT - 1:
                        between(k)
                return ins

            THREE = ((0, 0), (0, 1), (1, 0))
            TWO = ((0, 0), (1, 0))

            def block_product(blk, t, p, between=None):
                pe.wait_ge(mm_out, slot_free(t + NT * blk))
                product([ps[:, 2 * p + c, :] for c in range(2)],
                        lambda k, a: xnt[:, bass.ds(t, 1), k, a, :].rearrange("p o c -> p (o c)"),
                        wsl[blk % 2], TWO if blk == F else THREE, between).then_inc(mm_done, 1)

            def f_product(t, p):
                pe.wait_ge(xth_out, ready(t))
                pe.wait_ge(xtl_out, ready(t))
                block_product(F, t, p)

            for t in range(2):
                turn_x(t, t)
            pe.wait_ge(sign_done, KT)
            f_product(0, 0)
            pe.wait_ge(ones_set, 1)
            pe.wait_ge(asump_done, KT // 2 - 1)
            pe.wait_ge(asumv_done, KT // 2 - 1)
            for c in range(2):
                for s in range(2):
                    ins = nc.tensor.matmul(ps[:, 2 + c, :], ones, asum[s][:, c * HALF:(c + 1) * HALF],
                                           start=(s == 0), stop=(s == 1))
            ins.then_inc(alpha_sum, 1)
            turn_x(2, 0)
            pe.wait_ge(alpha_set, 1)
            f_product(1, 1)
            with pe.Fori(1, NT // 2 - 1) as j:
                for p in range(2):
                    turn_x(j * 2 + p + 1, 1 - p)
                    f_product(j * 2 + p, p)
            turn_x(NT - 1, 1)
            f_product(NT - 2, 0)
            f_product(NT - 1, 1)

            def turn_qk(q, p):
                pe.wait_ge(lo_done, ready(q))
                pe.wait_ge(qt_out, slot_free(q))
                for m in range(HEADS // 2):
                    src = qhl[p][:, 2 * m:2 * m + 2, :, :].rearrange("p h s d -> p (h s d)")
                    ins = nc.tensor.transpose(bank16(4 + 2 * p + m // 8)[:, (m % 8) * P:(m % 8 + 1) * P],
                                              src, idh)
                ins.then_inc(qt_done, 1)

            for blk in (Q, K):
                pe.wait_ge(w_lo, ready(NT * blk - 1))

                def step(t, p, j, first=False):
                    block_product(blk, t, p)
                    if blk == K or not first:
                        turn_qk(t + (NT * (blk - 1) - 1), 1 - p)

                tile_loop(pe, step)

            def nat(n, c):
                s = n[1] % STACKS
                pe.wait_ge(nat_out, step_no(n, NB, slot_free(nat_item(n, c))))
                for i, key, width, col in NAT[c]:
                    dst = ps[:, NATB[nat_item(n, c) % RB], col:col + width]
                    diagonal = key + width == P * (i + 1)
                    ins = nc.tensor.matmul(dst, qs[s][:, i * P:(i + 1) * P], ks[s][:, key:key + width],
                                           start=True, stop=not diagonal)
                    if diagonal:
                        ins = nc.tensor.matmul(dst[:, width - P:width], idb, mnat, start=False, stop=True)
                ins.then_inc(nat_done, 1)

            def row(n):
                pe.wait_ge(negm_done, step_no(n) + 1)
                pe.wait_ge(nat_out, step_no(n, NB, slot_free(row_item(n))))
                nc.tensor.transpose(bank16(NATB[row_item(n) % RB])[0:QT, 0:P], negm[n[1] % 2][:, 0:QT], idh)\
                  .then_inc(nat_done, 1)

            def head_loaded(n):
                pe.wait_ge(head_ld[n[1] % STACKS], n[0] * (16 * 6) + (n[1] // STACKS + 1) * 16 * 6)

            pe.wait_ge(w_lo, ready(NT * V - 1))
            NAT_BESIDE = [[c for c in range(len(NAT)) if c * (KT - 1) // len(NAT) == k]
                          for k in range(KT)]

            def v_step(t, p, j, edge):
                if edge not in (NT - 2, NT - 1):
                    block_product(V, t, p)
                    if edge == 0:
                        turn_qk(2 * NT - 1, 1)
                    return
                r = edge - (NT - 2)
                if r == 0:
                    pe.wait_ge(extra_ld, 16 * 2 * STACKS)
                    pe.wait_ge(qt_out, ready(NT * 2 - 1))
                head_loaded((0, r))

                def between(k):
                    for c in NAT_BESIDE[k]:
                        if c == ROW_AT and r == 1:
                            row((0, 0))
                        nat((0, r), c)

                block_product(V, t, p, between)

            staggered_loop(pe, v_step)

            def scores(n, c):
                s = n[1] % STACKS
                t, q0, w = SC[c]
                pe.wait_ge(exp_done, step_no(n, NS, slot_free(c)))
                dst = ps[:, SCB[c % RB], q0 % HALF:q0 % HALF + w]
                diagonal = q0 == P * t
                ins = nc.tensor.matmul(dst, ks[s][:, t * P:(t + 1) * P], qs[s][:, q0:q0 + w],
                                       start=True, stop=not diagonal)
                if diagonal:
                    ins = nc.tensor.matmul(dst[:, 0:P], idb, mtr, start=False, stop=True)
                ins.then_inc(st_done, 1)

            def with_v(n, i):
                p, b, h = n[1] % 2, n[1] % 2, n[0] * 2 + n[1] // 2
                half = i // 4
                end = n[1] >= STEPS - 2
                for low_done, tiles in (((plp_done, POOL_END), (plv_done, DVE_END)) if end else
                                        ((plp_done, POOL_T), (plv_done, DVE_T))):
                    if i in tiles:
                        before = n[1] - (STEPS - 2) if end else 0
                        pe.wait_ge(low_done, step_no((n[0], n[1] - before), 4,
                                                     before * len(tiles) + tiles.index(i) + 1))
                if i % 4 == 0:
                    pe.wait_ge(raw_out, step_no(n, 2, slot_free(half)))
                dst = ps[:, PVB[half], (i % 4) * VW:(i % 4 + 1) * VW]
                for t in range(i + 1):
                    at = OFF[t] + P * (i - t)
                    rhs = vtile[b * QT + t][:, bass.ds(h, 1), :].rearrange("p o c -> p (o c)")
                    for part in (ph[p], pl[p]):
                        ins = nc.tensor.matmul(dst, part[:, at:at + P], rhs,
                                               start=(t == 0 and part is ph[p]),
                                               stop=(t == i and part is pl[p]))
                if i % 4 == 3:
                    ins.then_inc(pv_done, 1)

            PV_AFTER = {1: 0, 2: 1, 3: 2, 4: 3, 6: 4, 8: 5, 9: 6, 10: 7}

            def b_step(n, first=False, last=False, final=False):
                nxt, prv = (n[0], n[1] + 2), (n[0], n[1] - 1)
                pe.wait_ge(r_ld[n[1] % 2], n[0] * 32 + stored(n[1] // 2 + 1))
                if not last:
                    head_loaded(nxt)
                for c in range(NS):
                    scores(n, c)
                    if c == ROW_AT and not final:
                        row((n[0], n[1] + 1))
                    if c < len(NAT) and not last:
                        nat(nxt, c)
                    if c in PV_AFTER and not first:
                        with_v(prv, PV_AFTER[c])

            pe.wait_ge(mm_out, ready(NT * 4 - 1))
            b_step((0, 0), first=True)
            pe.wait_ge(v_ld[0], 16 * 3)
            b_step((0, 1))
            pe.wait_ge(v_ld[1], 16 * 3)
            with pe.Fori(0, STEPS // 4 - 1) as i:
                for r in range(4):
                    b_step((i, 2 + r))
            b_step((0, STEPS - 2), last=True)
            b_step((0, STEPS - 1), last=True, final=True)
            for i in range(QT):
                with_v((0, STEPS - 1), i)

            def turn_o(t, p):
                pe.wait_ge(ol_done, ready(t))
                pe.wait_ge(oth_out, slot_free(t))
                pe.wait_ge(otl_out, slot_free(t))
                for c, part in enumerate((oh[p], ol[p])):
                    for k in range(KT):
                        ins = nc.tensor.transpose(bank16(4 + 2 * p + c)[:, k * P:(k + 1) * P],
                                                  part[:, k * P:(k + 1) * P], idh)
                ins.then_inc(ott_done, 1)

            def out_product(t, p):
                pe.wait_ge(oth_out, ready(t))
                pe.wait_ge(otl_out, ready(t))
                pe.wait_ge(c_out, slot_free(t))
                product([ps[:, 2 * p + c, :] for c in range(2)], lambda k, a: ot[p][:, k, a, :],
                        wo, THREE).then_inc(c_done, 1)

            def c_step(t, p, j, edge):
                turn_o(t, p)
                if edge == 1:
                    pe.wait_ge(raw_out, ready(2 * STEPS - 1))
                if edge != 0:
                    out_product(t - 1, 1 - p)

            pe.wait_ge(exp_done, ready(NS * STEPS - 1, RB))
            pe.wait_ge(nat_out, ready(NB * STEPS - 1, RB))
            staggered_loop(pe, c_step)
            out_product(NT - 1, 1)


_INS = ["L0_attn_hidden_states", "L0_attn_Wqkv", "L0_attn_Wout", "L0_ffn_weight_real", "L0_ffn_bias",
        "L0_attn_q_ln_w", "L0_attn_q_ln_b", "L0_attn_k_ln_w", "L0_attn_k_ln_b"]


def _constants():
    import numpy as np

    eye = np.eye(P)
    later = np.arange(P)[None, :] > np.arange(P)[:, None]
    nat = np.where(later, -1e30, 0.0)
    q_extra = np.zeros((DH, SEQ), np.float16)
    q_extra[1:4] = 1.0
    slopes = 1.0 / np.power(2.0, np.arange(1, HEADS + 1, dtype=np.float32) * (8.0 / HEADS))
    rest = slopes[:, None].astype(np.float64) * (np.arange(SEQ) - SEQ // 2)[None, :] * np.sqrt(float(DH))
    k_extra = np.zeros((HEADS, 4, SEQ), np.float16)
    k_extra[:, 0] = 1.0
    for r in range(1, 4):
        k_extra[:, r] = rest.astype(np.float16)
        rest = rest - k_extra[:, r].astype(np.float64)

    def bf(v):
        return (v.astype(np.float32).view(np.uint32) >> 16).astype(np.uint16)

    return {"ident_h": eye.astype(np.float16), "ident_b": bf(eye), "mask_nat": bf(nat),
            "mask_tr": bf(nat.T.copy()), "q_extra": q_extra, "k_extra": k_extra}


def kernel(**inputs):
    import numpy as np
    import concourse.bacc as bacc
    from concourse.bass_utils import run_bass_kernel_spmd

    a = {n: np.ascontiguousarray(inputs[n]) for n in _INS}
    shape = a["L0_attn_hidden_states"].shape
    arrays = {
        "x": a["L0_attn_hidden_states"].reshape(TOK, DM),
        "wqkv_t": np.ascontiguousarray(a["L0_attn_Wqkv"].T),
        "wout_t": np.ascontiguousarray(a["L0_attn_Wout"].T),
        "wffn_t": np.ascontiguousarray(a["L0_ffn_weight_real"].T),
        "ffn_bias": a["L0_ffn_bias"],
        "q_w": a["L0_attn_q_ln_w"], "q_b": a["L0_attn_q_ln_b"],
        "k_w": a["L0_attn_k_ln_w"], "k_b": a["L0_attn_k_ln_b"],
        **_constants(),
    }
    nc = bacc.Bacc("TRN2", target_bir_lowering=False, num_devices=1)
    args = [nc.dram_tensor(f"in_{n}", v.shape, mybir.dt.from_np(v.dtype), kind="ExternalInput").ap()
            for n, v in arrays.items()]
    out = nc.dram_tensor("out_dram", (TOK, DM), F32, kind="ExternalOutput").ap()
    build_program(nc, *args, out)
    r = run_bass_kernel_spmd(nc, [{f"in_{n}": v for n, v in arrays.items()}], core_ids=[0])
    return r.results[0]["out_dram"].reshape(shape)
```
